# Optimizing a Trainium2 kernel written in Bass

```python
import numpy as np
import jax
import jax.numpy as jnp

def _softmax(x, axis=-1):
    return jax.nn.softmax(x, axis=axis)

def _gelu(x):
    return jax.nn.gelu(x, approximate=True)

def _silu(x):
    return jax.nn.silu(x)

def _sigmoid(x):
    return jax.nn.sigmoid(x)

def _layernorm(x, axis=-1, eps=1e-05):
    m = jnp.mean(x, axis=axis, keepdims=True)
    v = jnp.var(x, axis=axis, keepdims=True)
    return (x - m) / jnp.sqrt(v + eps)

def _scatter_add(tgt, idx, src, axis=0):
    return tgt.at[idx].add(src)

def _segment_sum(src, seg, n):
    return jax.ops.segment_sum(src, seg, n)
kernel_name = 'mk_adj_ffn_d1_adj_r2_55b7b3'

def setup_inputs(seed: int=0):
    np.random.seed(seed)
    _w = jnp.asarray

    def _rec_inputs():
        import jax
        import jax.numpy as jnp
        _gk = jax.random.key(seed)
        x = 7.22e-05 + 1 * jax.random.normal(jax.random.fold_in(_gk, 1), (1354, 512), jnp.float32)
        _a = jax.random.bernoulli(jax.random.fold_in(_gk, 2), 0.0014771, (1354, 1354))
        _a = jnp.logical_or(_a, jnp.swapaxes(_a, -1, -2))
        _a = jnp.logical_or(_a, jnp.eye(1354, dtype=bool))
        adj = _a.astype(jnp.int32)
        return (x, adj)
    x, adj = _rec_inputs()

    def _L0_gnn_setup():
        import jax, jax.numpy as jnp
        import numpy as np
        N = 4096
        F_IN = 512
        F_OUT = 512
        ALPHA = 0.2
        NEG_INF = -9000000000000000.0
        key = jax.random.key(seed)
        k0, k1, k2, k3, k4 = jax.random.split(key, 5)
        input = jax.random.normal(k0, (N, F_IN), dtype=jnp.float32)
        W = jax.random.normal(k1, (F_IN, F_OUT), dtype=jnp.float32) * np.sqrt(2.0 / (F_IN + F_OUT)).astype(np.float32)
        a1 = jax.random.normal(k2, (F_OUT, 1), dtype=jnp.float32) * 0.05
        a2 = jax.random.normal(k3, (F_OUT, 1), dtype=jnp.float32) * 0.05
        adj = jax.random.randint(k4, (N, N), 0, 2, dtype=jnp.int32)
        return {'input': input, 'adj': adj, 'W': W, 'a1': a1, 'a2': a2}
    _L0_gnn_all = _L0_gnn_setup()
    _L0_gnn_in = {k: v for k, v in _L0_gnn_all.items() if k in ('W', 'a1', 'a2')}
    del _L0_gnn_all

    def _L0_ffn_setup():
        import jax, jax.numpy as jnp
        import numpy as np
        key = jax.random.key(seed)
        ks = jax.random.split(key, 5)
        B, T, D, E = (4, 1024, 512, 8)
        inputs = jax.random.normal(ks[0], (B, T, D), dtype=jnp.float32)
        Wr = jax.random.normal(ks[1], (D, E), dtype=jnp.float32) * 0.02
        br = jnp.zeros((E,), dtype=jnp.float32)
        W1 = jax.random.normal(ks[2], (E, D, D), dtype=jnp.float32) * 0.02
        b1 = jnp.zeros((E, D), dtype=jnp.float32)
        W2 = jax.random.normal(ks[3], (E, D, D), dtype=jnp.float32) * 0.02
        b2 = jnp.zeros((E, D), dtype=jnp.float32)
        return {'inputs': inputs, 'Wr': Wr, 'br': br, 'W1': W1, 'b1': b1, 'W2': W2, 'b2': b2}
    _L0_ffn_all = _L0_ffn_setup()
    _L0_ffn_in = {k: v for k, v in _L0_ffn_all.items() if k in ('Wr', 'br', 'W1', 'b1', 'W2', 'b2')}
    del _L0_ffn_all
    return {'x': x, 'adj': adj, 'L0_gnn_W': _L0_gnn_in['W'], 'L0_gnn_a1': _L0_gnn_in['a1'], 'L0_gnn_a2': _L0_gnn_in['a2'], 'L0_ffn_Wr': _L0_ffn_in['Wr'], 'L0_ffn_br': _L0_ffn_in['br'], 'L0_ffn_W1': _L0_ffn_in['W1'], 'L0_ffn_b1': _L0_ffn_in['b1'], 'L0_ffn_W2': _L0_ffn_in['W2'], 'L0_ffn_b2': _L0_ffn_in['b2']}

def reference(x, adj, L0_gnn_W, L0_gnn_a1, L0_gnn_a2, L0_ffn_Wr, L0_ffn_br, L0_ffn_W1, L0_ffn_b1, L0_ffn_W2, L0_ffn_b2):
    import jax
    import jax.numpy as jnp

    def _L0_gnn_ref(input, adj, W, a1, a2):
        import jax, jax.numpy as jnp
        import numpy as np
        N = 4096
        F_IN = 512
        F_OUT = 512
        ALPHA = 0.2
        NEG_INF = -9000000000000000.0
        h = input @ W
        f1 = h @ a1
        f2 = h @ a2
        e = jax.nn.leaky_relu(f1 + f2.T, negative_slope=ALPHA)
        neg = jnp.asarray(NEG_INF, dtype=e.dtype)
        scores = jnp.where(adj > 0, e, neg)
        attention = jax.nn.softmax(scores, axis=1)
        h_prime = attention @ h
        return jax.nn.relu(h_prime)

    def _L0_ffn_ref(inputs, Wr, br, W1, b1, W2, b2):
        import jax, jax.numpy as jnp
        import numpy as np
        B, T, D = inputs.shape
        E = Wr.shape[1]
        x = inputs.reshape(B * T, D)
        N = x.shape[0]
        C = N // E
        logits = x @ Wr + br
        probs = jax.nn.softmax(logits, axis=-1)
        gate = jnp.max(probs, axis=-1, keepdims=True)
        idx = jnp.argmax(probs, axis=-1)
        mask = jax.nn.one_hot(idx, E, dtype=jnp.float32)
        pos = (jnp.cumsum(mask, axis=0) * mask).astype(jnp.int32)
        mask = mask * (pos < C).astype(jnp.float32)
        mask_flat = jnp.sum(mask, axis=-1, keepdims=True)
        gate = gate * mask_flat
        combine = (gate * mask_flat * jax.nn.one_hot(idx, E, dtype=jnp.float32))[..., None] * jax.nn.one_hot(pos, C, dtype=jnp.float32)
        dispatch = combine
        expert_in = jnp.einsum('nd,nec->ecd', x, dispatch)
        h = jax.nn.relu(jnp.einsum('ecd,edf->ecf', expert_in, W1) + b1[:, None, :])
        eo = jnp.einsum('ecf,efd->ecd', h, W2) + b2[:, None, :]
        out = jnp.einsum('ecd,nec->nd', eo, combine)
        return out.reshape(B, T, D)
    x = x + _L0_gnn_ref(_layernorm(x, axis=-1), adj, L0_gnn_W, L0_gnn_a1, L0_gnn_a2)
    x = x + _L0_ffn_ref(_layernorm(x, axis=-1)[None], L0_ffn_Wr, L0_ffn_br, L0_ffn_W1, L0_ffn_b1, L0_ffn_W2, L0_ffn_b2)[0]
    return x

_drawn_inputs = setup_inputs


def setup_inputs(seed=0):
    import zlib

    import numpy as np

    out = dict(_drawn_inputs(seed))
    spreads = {'L0_ffn_br': (0.0, 0.517), 'L0_ffn_b1': (0.0, 0.8), 'L0_ffn_b2': (0.0, 0.41)}
    factors = {'L0_ffn_Wr': 2.811, 'L0_ffn_W1': 8.0, 'L0_ffn_W2': 5.857}
    for name, (base, spread) in spreads.items():
        noise = np.random.default_rng([zlib.crc32(name.encode()), seed]).standard_normal(out[name].shape)
        drawn = base * np.exp(spread * noise) if base else spread * noise
        out[name] = jnp.asarray(drawn.astype(out[name].dtype))
    for name, factor in factors.items():
        out[name] = (out[name] * factor).astype(out[name].dtype)
    return out
```

```python
from contextlib import ExitStack

import concourse.bass as bass
from concourse import mybir

ALU = mybir.AluOpType
ACT = mybir.ActivationFunctionType
AX = mybir.AxisListType
F32 = mybir.dt.float32
F32R = mybir.dt.float32r
BF16 = mybir.dt.bfloat16
I32 = mybir.dt.int32
U32 = mybir.dt.uint32

P = 128
MASKED = -9e15
SLOPE = 0.2
EPS = 1e-5
LEAST = -3.0e38


def gat_moe(nc, x, adj, W, a1, a2, Wr, br, W1, b1, W2, b2, out):
    N, D = x.shape
    E = Wr.shape[1]
    KC = D // P
    NT = (N + P - 1) // P
    TAIL = N - (NT - 1) * P
    CAP = N // E - 1
    CAP2 = CAP - P
    SLOTS = E * CAP
    ROW = D + 2
    NOWHERE = 5000
    H0 = D // 2
    WC = D + 2
    BANKS3 = (0, 4, 8, NT)
    assert D == 512 and E == 8 and P < CAP <= 2 * P and NT == 11 and TAIL < P

    x1_d = nc.dram_tensor("x1_rows", [N, D], F32).ap()
    disp = nc.dram_tensor("dispatched", [SLOTS + N, ROW], F32).ap()

    def rows(t):
        return TAIL if isinstance(t, int) and t == NT - 1 else P

    def there(t, n=NT):
        return not isinstance(t, int) or 0 <= t < n

    with ExitStack() as ctx:
        def sb(name, shape, dt=F32):
            return ctx.enter_context(nc.sbuf_tensor(name, shape, dt))

        def sem(name):
            return ctx.enter_context(nc.semaphore(name))

        x_all = sb("x_all", [P, NT, D])
        h_hi = sb("h_hi", [P, NT, D], F32R)
        h_lo = sb("h_lo", [P, NT, D], F32R)
        w_raw = sb("w_raw", [P, KC, D])
        w_hi = sb("w_hi", [P, KC, WC], F32R)
        w_lo = sb("w_lo", [P, KC, WC], F32R)
        xn = sb("xn", [P, 2, D])
        xt_hi = sb("xt_hi", [P, 2, KC, P], F32R)
        xt_lo = sb("xt_lo", [P, 2, KC, P], F32R)
        f2b = sb("f2b", [P, N])
        adj_s = sb("adj_s", [P, 2, N], I32)
        score = sb("score", [P, N])
        score2 = sb("score2", [P, N])
        prob = sb("prob", [P, 2, N])
        pt_hi = sb("pt_hi", [P, 2, NT, P], F32R)
        pt_lo = sb("pt_lo", [P, 2, NT, P], F32R)
        w1_s = sb("w1_s", [P, 2, KC, D])
        w2_s = sb("w2_s", [P, 2, KC, D])
        ident = sb("ident", [P, P])
        upto = sb("upto", [P, P], BF16)
        ones = sb("ones", [P, P], BF16)
        vecs = sb("vecs", [P, 4, D])
        a1_b, a2_b, wa2_b, junk = (vecs[:, i, :] for i in range(4))
        wa = sb("wa", [P, 2, KC])
        wr_s = sb("wr_s", [P, KC, E])
        br_b = sb("br_b", [P, E])
        b_cols = sb("b_cols", [P, 2, E * KC])
        half = sb("half", [P, 1])
        iota_e = sb("iota_e", [P, E])
        token1 = sb("token1", [P, NT])
        dump1 = sb("dump1", [P, NT])
        stat = sb("stat", [P, 6])
        mv = sb("mv", [P, 2, 2])
        ve = sb("ve", [P, 2, 1])
        rstd = sb("rstd", [P, 2, 1])
        stat2 = sb("stat2", [P, 6])
        mv2 = sb("mv2", [P, 2])
        ve2 = sb("ve2", [P, 1])
        rstd2 = sb("rstd2", [P, 1])
        f1 = sb("f1", [P, NT])
        f2_c = sb("f2_c", [P, 1])
        f2 = sb("f2", [P, NT])
        fmax = sb("fmax", [P, 1])
        zmax = sb("zmax", [P, 1])
        rmax = sb("rmax", [P, 1])
        off_a = sb("off_a", [P, 1])
        off_b = sb("off_b", [P, 1])
        rsum = sb("rsum", [P, 2, 1])
        rinv = sb("rinv", [P, 2, 1])
        logit = sb("logit", [P, E])
        nmax = sb("nmax", [P, 1])
        pe8 = sb("pe8", [P, E])
        zsum = sb("zsum", [P, 1])
        top8 = sb("top8", [P, E])
        idx8 = sb("idx8", [P, E], U32)
        zinv = sb("zinv", [P, 1])
        idxf = sb("idxf", [P, 2, 1])
        onehot = sb("onehot", [P, 2, E], BF16)
        counts = sb("counts", [P, E], BF16)
        junk8 = sb("junk8", [P, E])
        pos = sb("pos", [P, 1])
        fits = sb("fits", [P, 1])
        place = sb("place", [P, 1])
        place_d = sb("place_d", [P, 1])
        slot_f = sb("slot_f", [P, 1])
        slot = sb("slot", [P, 2, 1], U32)
        relu_s = w_raw[:, 0, :]
        b_rows = w_raw[0:E * KC, 1, 0:2 * P].rearrange("q (j p) -> q j p", j=2)
        row_s = vecs[:, :, :].rearrange("p i n -> p (i n)")[:, 0:2 * ROW].rearrange("p (i n) -> p i n", i=2)
        x2t = xn[:, :, :].rearrange("p i (c n) -> p i c n", c=KC)
        zeros = score2[:, 0:ROW]
        disp_s = score[:, 0:2 * ROW].rearrange("p (j n) -> p j n", j=2)
        disp_o = score2[:, 0:2 * ROW].rearrange("p (j n) -> p j n", j=2)
        dispatched = (disp_s, disp_o)
        gx_t = [prob[:, i, 0:KC * CAP].rearrange("p (c n) -> p c n", c=KC) for i in range(2)]
        hid = [adj_s[:, i, 0:KC * CAP].bitcast(F32).rearrange("p (c n) -> p c n", c=KC) for i in range(2)]
        eo_t = [adj_s[:, i, KC * CAP:2 * KC * CAP].bitcast(F32).rearrange("p (c n) -> p c n", c=KC)
                for i in range(2)]
        x1_g = w_raw[:, :, :].rearrange("p (i j) n -> p i j n", i=2)
        fin = vecs[:, :, :].rearrange("p (i j) n -> p i j n", i=2)
        emp = sb("emp", [P, 2])
        tokf = sb("tokf", [P, 2])
        dest = sb("dest", [P, 2, 2], U32)
        src = sb("src", [P, 2, 2], U32)

        banks = [ctx.enter_context(nc.psum_tensor(f"bank{i}", [P, 512], F32)) for i in range(8)]
        xt_ps = (banks[0], banks[1])
        h_ps = ((banks[2], banks[3]), (banks[4], banks[5]))
        row_ps = (banks[6], banks[7], banks[0])
        pt_ps = (banks[1], banks[2], banks[3])
        o_ps = (banks[4], banks[5])
        x2_ps, logit_ps, pos_ps = banks[6], banks[7], banks[0]
        gx_ps, hid_ps, eo_ps, y_ps = ((banks[0], banks[1]), (banks[2], banks[3]),
                                      (banks[4], banks[5]), (banks[6], banks[7]))

        s_x = [sem("s_x_even"), sem("s_x_odd")]
        s_w, s_a, s_small, s_bias = sem("s_w"), sem("s_a"), sem("s_small"), sem("s_bias")
        s_adj = [sem("s_adj0"), sem("s_adj1")]
        s_zero = sem("s_zero")
        s_w1 = [sem("s_w1_0"), sem("s_w1_1")]
        s_w2 = [sem("s_w2_0"), sem("s_w2_1")]
        s_const, s_fill, s_held = sem("s_const"), sem("s_fill"), sem("s_held")
        s_stat, s_mv, s_ve, s_rstd, s_xn = (sem(n) for n in ("s_stat", "s_mv", "s_ve", "s_rstd", "s_xn"))
        s_f2c = sem("s_f2c")
        s_f2, s_xt, s_xhi, s_xlo = (sem(n) for n in ("s_f2", "s_xt", "s_xhi", "s_xlo"))
        s_h, s_hhi, s_hlo = (sem(n) for n in ("s_h", "s_hhi", "s_hlo"))
        s_wa, s_whi, s_wa1, s_wlo, s_wa2t, s_wa2b = (
            sem(n) for n in ("s_wa", "s_whi", "s_wa1", "s_wlo", "s_wa2t", "s_wa2b"))
        s_row, s_f2b, s_bt, s_bc = (sem(n) for n in ("s_row", "s_f2b", "s_bt", "s_bc"))
        s_pen, s_fmax, s_zmax, s_rmax, s_off = (
            sem(n) for n in ("s_pen", "s_fmax", "s_zmax", "s_rmax", "s_off"))
        s_low, s_arg, s_prob, s_rinv = (sem(n) for n in ("s_low", "s_arg", "s_prob", "s_rinv"))
        s_pt = [sem(f"s_pt{b}") for b in range(3)]
        s_phi = [sem(f"s_phi{b}") for b in range(3)]
        s_plo = [sem(f"s_plo{b}") for b in range(3)]
        s_o, s_relu, s_x1 = sem("s_o"), sem("s_relu"), sem("s_x1")
        s_out = [sem("s_out0"), sem("s_out1")]
        s_stat2, s_mv2, s_ve2, s_rstd2, s_xn2 = (
            sem(n) for n in ("s_stat2", "s_mv2", "s_ve2", "s_rstd2", "s_xn2"))
        s_x2t, s_x2, s_logit = sem("s_x2t"), sem("s_x2"), sem("s_logit")
        s_lg, s_nmax, s_pe8, s_top, s_idx, s_idxf, s_onehot = (
            sem(n) for n in ("s_lg", "s_nmax", "s_pe8", "s_top", "s_idx", "s_idxf", "s_onehot"))
        s_zinv, s_gate, s_gx = sem("s_zinv"), sem("s_gate"), sem("s_gx")
        s_post, s_count, s_pos, s_fits, s_place, s_dist, s_slotf, s_slot = (
            sem(n) for n in ("s_post", "s_count", "s_pos", "s_fits", "s_place", "s_dist", "s_slotf", "s_slot"))
        s_scat = [sem("s_scat0"), sem("s_scat1")]
        s_in = [sem("s_in0"), sem("s_in1")]
        s_gt, s_gxt, s_hid, s_hidv, s_eo, s_eov, s_y, s_fin = (
            sem(n) for n in ("s_gt", "s_gxt", "s_hid", "s_hidv", "s_eo", "s_eov", "s_y", "s_fin"))
        s_emp, s_tok, s_dest = sem("s_emp"), sem("s_tok"), sem("s_dest")
        s_x1g = [sem("s_x1g0"), sem("s_x1g1")]
        s_end = [sem("s_end0"), sem("s_end1")]

        def landed(t, par, each=16):
            return (t - par) * (each // 2) + each

        def after(eng, sem_, t, lag):
            if not isinstance(t, int) or t >= lag:
                eng.wait_ge(sem_, t - (lag - 1))

        def hold(eng, sem_, value):
            eng.wait_ge(sem_, value)
            eng.sem_inc(s_held, 1)

        def sweep(eng, step, lag, ahead, n):
            first, last = 2, (n - 1 - ahead) // 2 * 2
            for i in range(-ahead, first):
                step(i, i % 2)
            with eng.Fori(first // 2, last // 2) as pair:
                step(pair * 2, 0)
                step(pair * 2 + 1, 1)
            for i in range(last, n + lag):
                step(i, i % 2)

        block = ctx.enter_context(nc.Block())

        @block.sync
        def _(sp):
            def load_x(t, par):
                if not there(t):
                    return
                R = rows(t)
                if not isinstance(t, int) or t >= 2:
                    hold(sp, s_x[par], landed(t, par) - 16)
                if isinstance(t, int):
                    sp.dma_start(x_all[0:R, t, :], x[t * P:t * P + R, :]).then_inc(s_x[par], 16)
                else:
                    sp.dma_start(x_all[:, t, :], x[bass.ds(t * P, P), :]).then_inc(s_x[par], 16)

            sweep(sp, load_x, 0, 0, NT)
            sp.dma_start(wr_s[:, :, :], Wr.rearrange("(c p) e -> p c e", p=P)).then_inc(s_small, 16)
            sp.dma_start(br_b[:, :], br.partition_broadcast(P)).then_inc(s_small, 16)

            def load_adj(t, par):
                if not there(t):
                    return
                R = rows(t)
                after(sp, s_fmax, t, 2)
                if isinstance(t, int):
                    sp.dma_start(adj_s[0:R, par, :], adj[t * P:t * P + R, :]).then_inc(s_adj[par], 16)
                else:
                    sp.dma_start(adj_s[:, par, :], adj[bass.ds(t * P, P), :]).then_inc(s_adj[par], 16)

            def store_x1(t, par):
                if not there(t):
                    return
                R = rows(t)
                hold(sp,s_x1, t + 1)
                if not isinstance(t, int) or t >= 2:
                    hold(sp, s_out[par], landed(t, par, 32) - 32)
                for d in (out, x1_d):
                    sp.dma_start(d[bass.ds(t * P, R), :], x_all[0:R, t, :]).then_inc(s_out[par], 16)

            def load_expert(e, par):
                if isinstance(e, int):
                    v1, v2 = W1[e, :, :], W2[e, :, :]
                else:
                    v1 = W1[bass.ds(e, 1), :, :].rearrange("a k n -> (a k) n")
                    v2 = W2[bass.ds(e, 1), :, :].rearrange("a k n -> (a k) n")
                after(sp, s_hid, e, 2)
                sp.dma_start(w1_s[:, par, :, :], v1.rearrange("(c p) n -> p c n", p=P)).then_inc(s_w1[par], 16)
                after(sp, s_eo, e, 2)
                sp.dma_start(w2_s[:, par, :, :], v2.rearrange("(c p) n -> p c n", p=P)).then_inc(s_w2[par], 16)

            load_adj(0, 0)
            load_adj(1, 1)
            sp.wait_ge(s_fill, 3)
            ZP = SLOTS // 12
            sp.dma_start(disp[0:SLOTS, :].rearrange("(p j) n -> p j n", p=ZP),
                         zeros[0:ZP, :].unsqueeze(1).broadcast_to([ZP, 12, ROW])).then_inc(s_zero, 16)

            def tile(t, par):
                if there(t + 2) and not (isinstance(t, int) and t < 0):
                    load_adj(t + 2, par)
                store_x1(t - 1, 1 - par)

            for t in range(0, 2):
                tile(t, t % 2)
            load_expert(0, 0)
            load_expert(1, 1)
            with sp.Fori(1, 8 // 2) as pair:
                t = pair * 2
                tile(t, 0)
                tile(t + 1, 1)
            for t in range(8, NT + 1):
                tile(t, t % 2)

            def load_rows(e, par):
                after(sp, s_fin, e, 2)
                base = e * CAP
                d = dispatched[par]
                sp.dma_start(d[:, 0, :], disp[bass.ds(base, P), :]).then_inc(s_in[par], 16)
                sp.dma_start(d[0:CAP2, 1, :], disp[bass.ds(base + P, CAP2), :]).then_inc(s_in[par], 16)

            sp.wait_ge(s_scat[0], landed(10, 0))
            sp.wait_ge(s_scat[1], landed(9, 1))
            def expert(e, par):
                if not isinstance(e, int) or e >= 2:
                    load_expert(e, par)
                load_rows(e, par)

            sweep(sp, expert, 0, 0, E)
            sp.wait_ge(s_end[0], 32 * (E // 2))
            sp.wait_ge(s_end[1], 32 * (E // 2))

        @block.gpsimd
        def _(pool):
            pool.memset(ident[:, :], 0.0).then_inc(s_fill, 1)
            pool.memset(upto[:, :], 1.0).then_inc(s_fill, 1)
            pool.memset(zeros[:, :], 0.0).then_inc(s_fill, 1)
            pool.memset(half[:, :], -0.5).then_inc(s_const, 1)
            pool.wait_ge(s_fill, 2)
            pool.affine_select(out=ident[:, :], in_=ident[:, :], compare_op=ALU.not_equal, fill=1.0,
                               base=0, pattern=[[-1, P]], channel_multiplier=1).then_inc(s_const, 1)
            pool.affine_select(out=upto[:, :], in_=upto[:, :], compare_op=ALU.is_ge, fill=0.0,
                               base=0, pattern=[[1, P]], channel_multiplier=-1).then_inc(s_const, 1)
            pool.memset(w_hi[:, :, H0 + 1:H0 + 2].bitcast(F32), 0.0).then_inc(s_const, 1)
            pool.memset(w_lo[:, :, H0 + 1:H0 + 2].bitcast(F32), 0.0).then_inc(s_const, 1)
            pool.memset(ones[:, :], 1.0).then_inc(s_const, 1)
            pool.memset(counts[:, :], 0.0).then_inc(s_const, 1)
            pool.iota(iota_e[:, :], pattern=[[1, E]], base=0, channel_multiplier=0,
                      allow_small_or_imprecise_dtypes=True).then_inc(s_const, 1)
            pool.iota(token1[:, :], pattern=[[P, NT]], base=1, channel_multiplier=1,
                      allow_small_or_imprecise_dtypes=True).then_inc(s_const, 1)
            pool.iota(dump1[:, :], pattern=[[P, NT]], base=SLOTS + 1, channel_multiplier=1,
                      allow_small_or_imprecise_dtypes=True).then_inc(s_const, 1)
            pool.wait_ge(s_const, 1)

            def power(t, par):
                if not there(t):
                    return
                R = rows(t)
                pool.wait_ge(s_ve, t + 1)
                after(pool, s_xn, t, 2)
                pool.tensor_tensor(rstd[0:R, par, :], ve[0:R, par, :], half[0:R, :], ALU.pow).then_inc(s_rstd, 1)

            sweep(pool, power, 0, 0, NT)

            def residual(t, par):
                R = rows(t)
                pool.wait_ge(s_relu, t + 1)
                pool.tensor_tensor(x_all[0:R, t, :], x_all[0:R, t, :], relu_s[0:R, :], ALU.add).then_inc(s_x1, 1)

            def power2(t, par):
                R = rows(t)
                pool.wait_ge(s_ve2, t + 1)
                pool.tensor_tensor(rstd2[0:R, :], ve2[0:R, :], half[0:R, :], ALU.pow).then_inc(s_rstd2, 1)

            def scatter(t, par):
                R = rows(t)
                pool.wait_ge(s_slot, t + 1)
                hold(pool,s_gx, t + 1)
                pool.indirect_dma_start(disp, bass.IndirectOffsetOnAxis(ap=slot[0:R, par, :], axis=0),
                                        row_s[0:R, par, :], None).then_inc(s_scat[par], 16)

            def tile(t, par):
                if there(t - 2):
                    scatter(t - 2, par)
                if there(t - 1):
                    residual(t - 1, 1 - par)
                    power2(t - 1, 1 - par)

            pool.wait_ge(s_zero, 16)
            for t in range(1, 2):
                tile(t, t % 2)
            with pool.Fori(1, 8 // 2) as pair:
                t = pair * 2
                tile(t, 0)
                tile(t + 1, 1)
            for t in range(8, NT + 2):
                tile(t, t % 2)

            def gather_x1(e, par):
                hold(pool,s_dest, e + 1)
                for j, R in ((0, P), (1, CAP2)):
                    pool.indirect_dma_start(x1_g[0:R, par, j, :], None, x1_d,
                                            bass.IndirectOffsetOnAxis(ap=src[0:R, par, j:j + 1], axis=0)
                                            ).then_inc(s_x1g[par], 16)

            def scatter_out(e, par):
                hold(pool,s_fin, e + 1)
                for j, R in ((0, P), (1, CAP2)):
                    pool.indirect_dma_start(out, bass.IndirectOffsetOnAxis(ap=dest[0:R, par, j:j + 1], axis=0),
                                            fin[0:R, par, j, :], None, bounds_check=N - 1, oob_is_err=False
                                            ).then_inc(s_end[par], 16)

            pool.wait_ge(s_out[0], landed(10, 0, 32))
            pool.wait_ge(s_out[1], landed(9, 1, 32))

            def expert(e, par):
                if there(e, E):
                    scatter_out(e, par)
                if there(e + 1, E):
                    gather_x1(e + 1, 1 - par)

            sweep(pool, expert, 0, 1, E)

        @block.scalar
        def _(act):
            act.dma_start(w_raw[:, :, :], W.rearrange("(c p) n -> p c n", p=P)).then_inc(s_w, 16)
            act.dma_start(a1_b[:, :], a1.rearrange("n o -> (n o)").partition_broadcast(P)).then_inc(s_a, 16)
            act.dma_start(a2_b[:, :], a2.rearrange("n o -> (n o)").partition_broadcast(P)).then_inc(s_a, 16)
            act.wait_ge(s_w, 16)
            act.activation(w_hi[:, :, 0:H0], w_raw[:, :, 0:H0], ACT.Copy).then_inc(s_whi, 1)
            act.activation(w_hi[:, :, H0 + 2:WC], w_raw[:, :, H0:D], ACT.Copy).then_inc(s_whi, 1)

            def x_high(t, par):
                R = rows(t)
                act.wait_ge(s_xt, t + 1)
                after(act, s_h, t, 2)
                src_ = xt_ps[par][:, :].rearrange("p (c n) -> p c n", c=KC)
                act.activation(xt_hi[:, par, :, 0:R], src_[:, :, 0:R], ACT.Copy).then_inc(s_xhi, 1)

            def h_high(t, par):
                R = rows(t)
                act.wait_ge(s_h, t + 1)
                for j in range(2):
                    ins = act.activation(h_hi[0:R, t, j * H0:(j + 1) * H0], h_ps[par][j][0:R, 0:H0], ACT.Copy)
                ins.then_inc(s_hhi, 1)

            def tile1(t, par):
                if there(t + 1):
                    x_high(t + 1, 1 - par)
                if there(t):
                    h_high(t, par)
                if isinstance(t, int) and t == -1:
                    act.wait_ge(s_wa2t, 1)
                    act.activation(wa2_b[:, :], row_ps[0][:, :], ACT.Copy).then_inc(s_wa2b, 1)

            sweep(act, tile1, 0, 1, NT)

            act.wait_ge(s_wlo, 3)
            act.dma_start(b_rows[:, 0, :], b1.rearrange("e (c p) -> (e c) p", p=P)).then_inc(s_bias, 16)
            act.dma_start(b_rows[:, 1, :], b2.rearrange("e (c p) -> (e c) p", p=P)).then_inc(s_bias, 16)
            for b in range(3):
                lo, hi = BANKS3[b] * P, min(BANKS3[b + 1] * P, N)
                act.wait_ge(s_row, b + 1)
                act.activation(f2b[:, lo:hi], row_ps[b][:, 0:hi - lo], ACT.Copy).then_inc(s_f2b, 1)
            act.wait_ge(s_bt, 1)
            act.activation(b_cols[:, :, :], row_ps[2][:, 0:2 * E * KC].rearrange("p (j n) -> p j n", j=2),
                           ACT.Copy).then_inc(s_bc, 1)

            def relu_out(t, par):
                R = rows(t)
                act.wait_ge(s_o, t + 1)
                act.wait_ge(s_rinv, t + 1)
                after(act, s_x1, t, 1)
                act.activation(relu_s[0:R, :], o_ps[par][0:R, :], ACT.Relu, scale=rinv[0:R, par, :]
                               ).then_inc(s_relu, 1)

            def p_high(t, par, b):
                R = rows(t)
                act.wait_ge(s_pt[b], t + 1)
                after(act, s_o, t, 2)
                k0, k1 = BANKS3[b], BANKS3[b + 1]
                v = pt_ps[b][:, 0:(k1 - k0) * P].rearrange("p (k n) -> p k n", n=P)
                if b < 2:
                    act.activation(pt_hi[:, par, k0:k1, 0:R], v[:, :, 0:R], ACT.Copy).then_inc(s_phi[b], 1)
                else:
                    act.activation(pt_hi[:, par, k0:k1 - 1, 0:R], v[:, 0:k1 - k0 - 1, 0:R], ACT.Copy)
                    act.activation(pt_hi[0:TAIL, par, k1 - 1, 0:R], v[0:TAIL, k1 - k0 - 1, 0:R], ACT.Copy
                                   ).then_inc(s_phi[b], 1)

            def low_slope(t, par):
                R = rows(t)
                act.wait_ge(s_off, 2 * (t + 1))
                act.activation(score2[0:R, :], score[0:R, :], ACT.Identity, scale=SLOPE, bias=off_b[0:R, :]
                               ).then_inc(s_low, 1)

            def exps(t, par):
                R = rows(t)
                act.wait_ge(s_arg, t + 1)
                after(act, s_pt[2], t, 2)
                after(act, s_rinv, t, 2)
                act.activation(prob[0:R, par, :], score[0:R, :], ACT.Exp,
                               accum_out=rsum[0:R, par, :]).then_inc(s_prob, 1)

            def x2_copy(t, par):
                R = rows(t)
                act.wait_ge(s_x2t, t + 1)
                v = x2_ps[:, :].rearrange("p (c n) -> p c n", c=KC)
                act.activation(x2t[:, par, :, 0:R], v[:, :, 0:R], ACT.Copy).then_inc(s_x2, 1)

            def exp8(t, par):
                R = rows(t)
                act.wait_ge(s_nmax, t + 1)
                act.activation(pe8[0:R, :], logit[0:R, :], ACT.Exp, bias=nmax[0:R, :],
                               accum_out=zsum[0:R, :]).then_inc(s_pe8, 1)

            def gated(t, par):
                R = rows(t)
                act.wait_ge(s_gate, t + 1)
                act.activation(row_s[0:R, par, 0:D], row_s[0:R, par, 0:D], ACT.Copy,
                               scale=row_s[0:R, par, D:D + 1]).then_inc(s_gx, 1)

            def tile2(t, par):
                if there(t - 1):
                    relu_out(t - 1, 1 - par)
                if there(t + 1):
                    p_high(t + 1, 1 - par, 0)
                    p_high(t + 1, 1 - par, 1)
                if there(t + 2):
                    low_slope(t + 2, par)
                if there(t + 1):
                    p_high(t + 1, 1 - par, 2)
                if there(t - 1):
                    x2_copy(t - 1, 1 - par)
                if there(t + 2):
                    exps(t + 2, par)
                if there(t - 1):
                    exp8(t - 1, 1 - par)
                    gated(t - 1, 1 - par)

            act.wait_ge(s_zero, 16)
            sweep(act, tile2, 1, 2, NT)

            def gx_copy(e, par):
                act.wait_ge(s_gt, e + 1)
                after(act, s_hid, e, 2)
                for j in range(2):
                    ins = act.activation(gx_t[par][:, 2 * j:2 * j + 2, :],
                                         gx_ps[j][:, 0:2 * CAP].rearrange("p (c n) -> p c n", c=2), ACT.Copy)
                ins.then_inc(s_gxt, 1)

            def hid_relu(e, par):
                after(act, s_eo, e, 2)
                act.wait_ge(s_hid, e + 1)
                for c in range(KC):
                    ins = act.activation(hid[par][:, c, :], hid_ps[c // 2][:, (c % 2) * CAP:(c % 2 + 1) * CAP],
                                         ACT.Relu, bias=b_cols[:, 0, bass.ds(e * KC + c, 1)])
                ins.then_inc(s_hidv, 1)

            act.wait_ge(s_bc, 1)

            def expert(e, par):
                if there(e, E):
                    hid_relu(e, par)
                if there(e + 1, E):
                    gx_copy(e + 1, 1 - par)

            sweep(act, expert, 0, 1, E)

        @block.vector
        def _(dve):
            def stats(t, par):
                R = rows(t)
                dve.wait_ge(s_x[par], landed(t, par))
                dve.bn_stats(stat[0:R, :], x_all[0:R, t, :]).then_inc(s_stat, 1)
                hold(dve,s_stat, t + 1)
                dve.bn_aggr(mv[0:R, par, :], stat[0:R, :]).then_inc(s_mv, 1)
                dve.wait_ge(s_mv, t + 1)
                after(dve, s_rstd, t, 2)
                dve.tensor_scalar(ve[0:R, par, :], mv[0:R, par, 1:2], EPS, None, ALU.add).then_inc(s_ve, 1)

            def normal(t, par):
                R = rows(t)
                dve.wait_ge(s_rstd, t + 1)
                after(dve, s_xt, t, 2)
                after(dve, s_f2, t, 2)
                dve.tensor_scalar(xn[0:R, par, :], x_all[0:R, t, :], mv[0:R, par, 0:1], rstd[0:R, par, :],
                                  ALU.subtract, ALU.mult).then_inc(s_xn, 1)

            def x_low(t, par):
                R = rows(t)
                dve.wait_ge(s_xhi, t + 1)
                v = xt_ps[par][:, :].rearrange("p (c n) -> p c n", c=KC)
                dve.tensor_tensor(xt_lo[:, par, :, 0:R], v[:, :, 0:R], xt_hi[:, par, :, 0:R].bitcast(F32),
                                  ALU.subtract).then_inc(s_xlo, 1)

            def dot_f2(t, par):
                R = rows(t)
                dve.wait_ge(s_xn, t + 1)
                if isinstance(t, int) and t == 0:
                    dve.wait_ge(s_wa2b, 1)
                after(dve, s_f2c, t, 1)
                dve.tensor_tensor_reduce(junk[0:R, :], xn[0:R, par, :], wa2_b[0:R, :], 1.0, 0.0, ALU.mult,
                                         ALU.add, f2_c[0:R, :]).then_inc(s_f2, 1)
                dve.wait_ge(s_f2, t + 1)
                dve.tensor_copy(f2[0:R, bass.ds(t, 1)], f2_c[0:R, :]).then_inc(s_f2c, 1)

            def h_low(t, par):
                R = rows(t)
                dve.wait_ge(s_hhi, t + 1)
                for j in range(2):
                    dve.tensor_tensor(h_lo[0:R, t, j * H0:(j + 1) * H0], h_ps[par][j][0:R, 0:H0],
                                      h_hi[0:R, t, j * H0:(j + 1) * H0].bitcast(F32), ALU.subtract)
                dve.tensor_copy(f1[0:R, bass.ds(t, 1)], h_ps[par][0][0:R, H0:H0 + 1]).then_inc(s_hlo, 1)

            def weights1():
                dve.wait_ge(s_w, 16)
                dve.wait_ge(s_a, 32)
                for n, (j, c) in enumerate([(1, c) for c in range(KC)] + [(0, c) for c in range(KC)]):
                    if n:
                        dve.wait_ge(s_wa, n)
                    ab = (a1_b, a2_b)[j]
                    dve.tensor_tensor_reduce(junk[:, :], w_raw[:, c, :], ab[:, :], 1.0, 0.0, ALU.mult,
                                             ALU.add, wa[:, j, c:c + 1]).then_inc(s_wa, 1)
                dve.wait_ge(s_whi, 2)
                dve.tensor_tensor(w_lo[:, :, 0:H0], w_raw[:, :, 0:H0], w_hi[:, :, 0:H0].bitcast(F32),
                                  ALU.subtract).then_inc(s_wlo, 1)
                dve.tensor_tensor(w_lo[:, :, H0 + 2:WC], w_raw[:, :, H0:D], w_hi[:, :, H0 + 2:WC].bitcast(F32),
                                  ALU.subtract).then_inc(s_wlo, 1)
                dve.wait_ge(s_wa, 2 * KC)
                dve.tensor_copy(w_hi[:, :, H0], wa[:, 0, :]).then_inc(s_wa1, 1)
                dve.wait_ge(s_wa1, 1)
                dve.tensor_tensor(w_lo[:, :, H0], wa[:, 0, :], w_hi[:, :, H0].bitcast(F32),
                                  ALU.subtract).then_inc(s_wlo, 1)

            def tile1(t, par):
                if there(t + 2):
                    stats(t + 2, par)
                if there(t + 1):
                    x_low(t + 1, 1 - par)
                if there(t + 2):
                    normal(t + 2, par)
                if there(t):
                    h_low(t, par)
                if there(t + 1):
                    dot_f2(t + 1, 1 - par)
                if isinstance(t, int) and t == -2:
                    weights1()

            sweep(dve, tile1, 0, 2, NT)

            def scores(t, par):
                R = rows(t)
                dve.wait_ge(s_adj[par], landed(t, par))
                pen = adj_s[0:R, par, :].bitcast(F32)
                dve.tensor_scalar(pen, adj_s[0:R, par, :], 0.0, MASKED, ALU.is_le, ALU.mult).then_inc(s_pen, 1)
                after(dve, s_prob, t, 1)
                hold(dve, s_pen, t + 1)
                dve.tensor_tensor_reduce(score[0:R, :], pen, f2b[0:R, :], 1.0, LEAST, ALU.add, ALU.max,
                                         fmax[0:R, :]).then_inc(s_fmax, 1)
                f1t = f1[0:R, bass.ds(t, 1)]
                dve.wait_ge(s_fmax, t + 1)
                dve.tensor_tensor(zmax[0:R, :], fmax[0:R, :], f1t, ALU.add).then_inc(s_zmax, 1)
                dve.wait_ge(s_zmax, t + 1)
                dve.scalar_tensor_tensor(rmax[0:R, :], zmax[0:R, :], SLOPE, zmax[0:R, :], ALU.mult,
                                         ALU.max).then_inc(s_rmax, 1)
                dve.wait_ge(s_rmax, t + 1)
                dve.tensor_tensor(off_a[0:R, :], f1t, rmax[0:R, :], ALU.subtract).then_inc(s_off, 1)
                dve.scalar_tensor_tensor(off_b[0:R, :], f1t, SLOPE, rmax[0:R, :], ALU.mult,
                                         ALU.subtract).then_inc(s_off, 1)

            def argument(t, par):
                R = rows(t)
                dve.wait_ge(s_low, t + 1)
                dve.scalar_tensor_tensor(score[0:R, :], score[0:R, :], off_a[0:R, :], score2[0:R, :], ALU.add,
                                         ALU.max).then_inc(s_arg, 1)

            def sum_inverse(t, par):
                R = rows(t)
                dve.wait_ge(s_prob, t + 1)
                after(dve, s_relu, t, 2)
                dve.reciprocal(rinv[0:R, par, :], rsum[0:R, par, :]).then_inc(s_rinv, 1)

            def p_low(t, par, b):
                R = rows(t)
                dve.wait_ge(s_phi[b], t + 1)
                k0, k1 = BANKS3[b], BANKS3[b + 1]
                v = pt_ps[b][:, 0:(k1 - k0) * P].rearrange("p (k n) -> p k n", n=P)
                if b < 2:
                    dve.tensor_tensor(pt_lo[:, par, k0:k1, 0:R], v[:, :, 0:R],
                                      pt_hi[:, par, k0:k1, 0:R].bitcast(F32), ALU.subtract).then_inc(s_plo[b], 1)
                else:
                    dve.tensor_tensor(pt_lo[:, par, k0:k1 - 1, 0:R], v[:, 0:k1 - k0 - 1, 0:R],
                                      pt_hi[:, par, k0:k1 - 1, 0:R].bitcast(F32), ALU.subtract)
                    dve.tensor_tensor(pt_lo[0:TAIL, par, k1 - 1, 0:R], v[0:TAIL, k1 - k0 - 1, 0:R],
                                      pt_hi[0:TAIL, par, k1 - 1, 0:R].bitcast(F32), ALU.subtract
                                      ).then_inc(s_plo[b], 1)

            def stats2(t, par):
                R = rows(t)
                dve.wait_ge(s_x1, t + 1)
                dve.bn_stats(stat2[0:R, :], x_all[0:R, t, :]).then_inc(s_stat2, 1)
                hold(dve,s_stat2, t + 1)
                dve.bn_aggr(mv2[0:R, :], stat2[0:R, :]).then_inc(s_mv2, 1)
                dve.wait_ge(s_mv2, t + 1)
                dve.tensor_scalar(ve2[0:R, :], mv2[0:R, 1:2], EPS, None, ALU.add).then_inc(s_ve2, 1)

            def normal2(t, par):
                R = rows(t)
                dve.wait_ge(s_rstd2, t + 1)
                if not isinstance(t, int) or t >= 2:
                    dve.wait_ge(s_scat[par], landed(t, par) - 16)
                dve.tensor_scalar(row_s[0:R, par, 0:D], x_all[0:R, t, :], mv2[0:R, 0:1], rstd2[0:R, :],
                                  ALU.subtract, ALU.mult).then_inc(s_xn2, 1)

            def route(t, par):
                R = rows(t)
                dve.wait_ge(s_logit, t + 1)
                dve.tensor_tensor(logit[0:R, :], logit_ps[0:R, 0:E], br_b[0:R, :], ALU.add).then_inc(s_lg, 1)
                dve.wait_ge(s_lg, t + 1)
                dve.tensor_reduce(nmax[0:R, :], logit[0:R, :], AX.X, ALU.max, negate=True).then_inc(s_nmax, 1)
                hold(dve,s_pe8, t + 1)
                dve.max(top8[0:R, :], pe8[0:R, :]).then_inc(s_top, 1)
                dve.reciprocal(zinv[0:R, :], zsum[0:R, :]).then_inc(s_zinv, 1)
                hold(dve,s_top, t + 1)
                dve.max_index(idx8[0:R, :], top8[0:R, :], pe8[0:R, :]).then_inc(s_idx, 1)
                dve.wait_ge(s_zinv, t + 1)
                dve.tensor_tensor(row_s[0:R, par, D:D + 1], top8[0:R, 0:1], zinv[0:R, :], ALU.mult)
                dve.tensor_copy(row_s[0:R, par, D + 1:D + 2], token1[0:R, bass.ds(t, 1)]).then_inc(s_gate, 1)
                dve.wait_ge(s_idx, t + 1)
                dve.tensor_copy(idxf[0:R, par, :], idx8[0:R, 0:1]).then_inc(s_idxf, 1)
                dve.wait_ge(s_idxf, t + 1)
                dve.tensor_scalar(onehot[0:R, par, :], iota_e[0:R, :], idxf[0:R, par, :], None,
                                  ALU.is_equal).then_inc(s_onehot, 1)

            def places(t, par):
                R = rows(t)
                dve.wait_ge(s_post, t + 1)
                dve.tensor_tensor_reduce(junk8[0:R, :], pos_ps[0:R, 0:E], onehot[0:R, par, :], 1.0, 0.0,
                                         ALU.mult, ALU.add, pos[0:R, :]).then_inc(s_pos, 1)
                dve.tensor_tensor(counts[0:R, :], counts[0:R, :], onehot[0:R, par, :], ALU.add).then_inc(s_count, 1)
                dve.wait_ge(s_pos, t + 1)
                dve.tensor_scalar(fits[0:R, :], pos[0:R, :], float(CAP), None, ALU.is_le).then_inc(s_fits, 1)
                dve.scalar_tensor_tensor(place[0:R, :], idxf[0:R, par, :], float(CAP), pos[0:R, :], ALU.mult,
                                         ALU.add).then_inc(s_place, 1)
                dump = dump1[0:R, bass.ds(t, 1)]
                dve.wait_ge(s_place, t + 1)
                dve.tensor_tensor(place_d[0:R, :], place[0:R, :], dump, ALU.subtract).then_inc(s_dist, 1)
                dve.wait_ge(s_dist, t + 1)
                dve.scalar_tensor_tensor(slot_f[0:R, :], place_d[0:R, :], fits[0:R, :], dump, ALU.mult,
                                         ALU.add).then_inc(s_slotf, 1)
                dve.wait_ge(s_slotf, t + 1)
                dve.tensor_scalar(slot[0:R, par, :], slot_f[0:R, :], -1.0, None, ALU.add).then_inc(s_slot, 1)

            def tile2(t, par):
                if there(t + 1):
                    p_low(t + 1, 1 - par, 0)
                if there(t - 2):
                    places(t - 2, par)
                if there(t + 1):
                    p_low(t + 1, 1 - par, 1)
                if there(t + 2):
                    scores(t + 2, par)
                if there(t - 1):
                    stats2(t - 1, 1 - par)
                if there(t + 1):
                    p_low(t + 1, 1 - par, 2)
                if there(t - 1):
                    normal2(t - 1, 1 - par)
                if there(t + 2):
                    argument(t + 2, par)
                if there(t + 1):
                    sum_inverse(t + 1, 1 - par)
                if there(t - 1):
                    route(t - 1, 1 - par)

            dve.wait_ge(s_f2b, 3)
            dve.wait_ge(s_const, 10)
            dve.wait_ge(s_small, 32)
            sweep(dve, tile2, 2, 2, NT)

            def tokens(e, par):
                dve.wait_ge(s_in[par], landed(e, par, 32))
                d = dispatched[par]
                if not isinstance(e, int) or e >= 2:
                    dve.wait_ge(s_end[par], landed(e, par, 32) - 32)
                for j, R in ((0, P), (1, CAP2)):
                    ins = dve.tensor_scalar(emp[0:R, j:j + 1], d[0:R, j, D + 1:D + 2], 1.0, float(NOWHERE),
                                            ALU.is_lt, ALU.mult)
                    dve.tensor_scalar(tokf[0:R, j:j + 1], d[0:R, j, D + 1:D + 2], 1.0, -1.0,
                                      ALU.max, ALU.add)
                    ins = dve.tensor_scalar(src[0:R, par, j:j + 1], d[0:R, j, D + 1:D + 2], 1.0, -1.0,
                                            ALU.max, ALU.add)
                ins.then_inc(s_tok, 1)
                dve.wait_ge(s_tok, e + 1)
                for j, R in ((0, P), (1, CAP2)):
                    ins = dve.tensor_tensor(dest[0:R, par, j:j + 1], emp[0:R, j:j + 1], tokf[0:R, j:j + 1], ALU.add)
                ins.then_inc(s_dest, 1)

            def eo_bias(e, par):
                dve.wait_ge(s_eo, e + 1)
                after(dve, s_y, e, 2)
                for c in range(KC):
                    ins = dve.tensor_scalar(eo_t[par][:, c, :], eo_ps[c // 2][:, (c % 2) * CAP:(c % 2 + 1) * CAP],
                                            b_cols[:, 1, bass.ds(e * KC + c, 1)], None, ALU.add)
                ins.then_inc(s_eov, 1)

            def final(e, par):
                dve.wait_ge(s_y, e + 1)
                dve.wait_ge(s_x1g[par], landed(e, par, 32))
                for j, R in ((0, P), (1, CAP2)):
                    ins = dve.scalar_tensor_tensor(fin[0:R, par, j, :], y_ps[j][0:R, :],
                                                   dispatched[par][0:R, j, D:D + 1], x1_g[0:R, par, j, :],
                                                   ALU.mult, ALU.add)
                ins.then_inc(s_fin, 1)

            def expert(e, par):
                if there(e, E):
                    eo_bias(e, par)
                    final(e, par)
                if there(e + 1, E):
                    tokens(e + 1, 1 - par)

            dve.wait_ge(s_bc, 1)
            sweep(dve, expert, 0, 1, E)

        @block.tensor
        def _(pe):
            pe.wait_ge(s_const, 2)

            def x_turn(t, par):
                R = rows(t)
                pe.wait_ge(s_xn, t + 1)
                after(pe, s_xlo, t, 2)
                for c in range(KC):
                    ins = pe.transpose(xt_ps[par][:, c * P:c * P + R], xn[0:R, par, c * P:(c + 1) * P],
                                       ident[0:R, 0:R])
                ins.then_inc(s_xt, 1)

            def h_product(t, par):
                R = rows(t)
                pe.wait_ge(s_xlo, t + 1)
                after(pe, s_hlo, t, 2)
                parts = ((xt_lo, w_hi), (xt_hi, w_lo), (xt_hi, w_hi))
                for n, (a, w) in enumerate(parts):
                    for c in range(KC):
                        for j, (c0, c1) in enumerate(((0, H0 + 2), (H0 + 2, WC))):
                            ins = pe.matmul(h_ps[par][j][0:R, 0:c1 - c0], a[:, par, c, 0:R], w[:, c, c0:c1],
                                            start=(n == 0 and c == 0), stop=(n == 2 and c == KC - 1))
                ins.then_inc(s_h, 1)

            def tile1(t, par):
                if there(t + 1):
                    x_turn(t + 1, 1 - par)
                if isinstance(t, int) and t == -1:
                    pe.wait_ge(s_wa, KC)
                    for c in range(KC):
                        ins = pe.matmul(row_ps[0][:, c * P:(c + 1) * P], wa[:, 1, c:c + 1].broadcast_to([P, P]),
                                        ident[:, :], start=True, stop=True)
                    ins.then_inc(s_wa2t, 1)
                    pe.wait_ge(s_wlo, 3)
                    pe.wait_ge(s_const, 5)
                if there(t):
                    h_product(t, par)

            sweep(pe, tile1, 0, 1, NT)

            pe.wait_ge(s_f2c, NT)
            pe.wait_ge(s_wa2b, 1)
            for b in range(3):
                for t in range(BANKS3[b], BANKS3[b + 1]):
                    R = rows(t)
                    o = (t - BANKS3[b]) * P
                    ins = pe.matmul(row_ps[b][:, o:o + R], f2[0:R, t:t + 1].broadcast_to([R, P]), ident[0:R, 0:R],
                                    start=True, stop=True)
                ins.then_inc(s_row, 1)
            pe.wait_ge(s_bias, 32)
            pe.wait_ge(s_f2b, 3)
            for j in range(2):
                ins = pe.transpose(row_ps[2][:, j * E * KC:(j + 1) * E * KC], b_rows[:, j, :],
                                   ident[0:E * KC, 0:E * KC])
            ins.then_inc(s_bt, 1)

            def p_turn(t, par, b):
                R = rows(t)
                pe.wait_ge(s_prob, t + 1)
                after(pe, s_plo[b], t, 1)
                for k in range(BANKS3[b], BANKS3[b + 1]):
                    K = rows(k)
                    o = (k - BANKS3[b]) * P
                    ins = pe.transpose(pt_ps[b][0:K, o:o + R], prob[0:R, par, k * P:k * P + K], ident[0:R, 0:R])
                ins.then_inc(s_pt[b], 1)

            def attend(t, par, b):
                R = rows(t)
                pe.wait_ge(s_plo[b], t + 1)
                if b == 0:
                    after(pe, s_relu, t, 2)
                for k in range(BANKS3[b], BANKS3[b + 1]):
                    K = rows(k)
                    for n, (p, h) in enumerate(((pt_lo, h_hi), (pt_hi, h_lo), (pt_hi, h_hi))):
                        ins = pe.matmul(o_ps[par][0:R, :], p[0:K, par, k, 0:R], h[0:K, k, :],
                                        start=(k == 0 and n == 0), stop=(k == NT - 1 and n == 2))
                if b == 2:
                    ins.then_inc(s_o, 1)

            def x2_turn(t, par):
                R = rows(t)
                pe.wait_ge(s_xn2, t + 1)
                after(pe, s_x2, t, 1)
                for c in range(KC):
                    ins = pe.transpose(x2_ps[:, c * P:c * P + R], row_s[0:R, par, c * P:(c + 1) * P],
                                       ident[0:R, 0:R])
                ins.then_inc(s_x2t, 1)

            def logits(t, par):
                R = rows(t)
                pe.wait_ge(s_x2, t + 1)
                after(pe, s_lg, t, 1)
                for c in range(KC):
                    ins = pe.matmul(logit_ps[0:R, 0:E], x2t[:, par, c, 0:R], wr_s[:, c, :],
                                    start=(c == 0), stop=(c == KC - 1))
                ins.then_inc(s_logit, 1)

            def positions(t, par):
                R = rows(t)
                pe.wait_ge(s_onehot, t + 1)
                after(pe, s_count, t, 1)
                pe.matmul(pos_ps[0:R, 0:E], upto[0:R, 0:R], onehot[0:R, par, :], start=True, stop=False)
                pe.matmul(pos_ps[0:R, 0:E], ones[:, 0:R], counts[:, :], start=False, stop=True).then_inc(s_post, 1)

            def tile2(t, par):
                if there(t + 1):
                    p_turn(t + 1, 1 - par, 0)
                if there(t):
                    attend(t, par, 0)
                if there(t - 2):
                    positions(t - 2, par)
                if there(t + 1):
                    p_turn(t + 1, 1 - par, 1)
                if there(t):
                    attend(t, par, 1)
                if there(t + 1):
                    p_turn(t + 1, 1 - par, 2)
                if there(t - 1):
                    x2_turn(t - 1, 1 - par)
                if there(t):
                    attend(t, par, 2)
                if there(t - 1):
                    logits(t - 1, 1 - par)

            pe.wait_ge(s_bc, 1)
            pe.wait_ge(s_hlo, NT)
            pe.wait_ge(s_const, 10)
            pe.wait_ge(s_small, 32)
            sweep(pe, tile2, 2, 2, NT)

            def in_turn(e, par):
                pe.wait_ge(s_in[par], landed(e, par, 32))
                after(pe, s_gxt, e, 1)
                for c in range(KC):
                    o = (c % 2) * CAP
                    for j, R in ((0, P), (1, CAP2)):
                        ins = pe.transpose(gx_ps[c // 2][:, o + j * P:o + j * P + R],
                                           dispatched[par][0:R, j, c * P:(c + 1) * P], ident[0:R, 0:R])
                ins.then_inc(s_gt, 1)

            def layer(ps, w, v, f0=0, f1=KC):
                for f in range(f0, f1):
                    for c in range(KC):
                        ins = pe.matmul(ps[f // 2][:, (f % 2) * CAP:(f % 2 + 1) * CAP],
                                        w[:, c, f * P:(f + 1) * P], v[:, c, :], start=(c == 0), stop=(c == KC - 1))
                return ins

            def first_layer(e, par):
                pe.wait_ge(s_w1[par], landed(e, par))
                pe.wait_ge(s_gxt, e + 1)
                after(pe, s_hidv, e, 1)
                layer(hid_ps, w1_s[:, par, :, :], gx_t[par]).then_inc(s_hid, 1)

            def second_layer(e, par, half):
                if half == 0:
                    pe.wait_ge(s_w2[par], landed(e, par))
                    pe.wait_ge(s_hidv, e + 1)
                    after(pe, s_eov, e, 1)
                ins = layer(eo_ps, w2_s[:, par, :, :], hid[par], half * KC // 2, (half + 1) * KC // 2)
                if half == 1:
                    ins.then_inc(s_eo, 1)

            def out_turn(e, par):
                pe.wait_ge(s_eov, e + 1)
                after(pe, s_fin, e, 1)
                for j, R in ((0, P), (1, CAP2)):
                    for c in range(KC):
                        ins = pe.transpose(y_ps[j][0:R, c * P:(c + 1) * P], eo_t[par][:, c, j * P:j * P + R],
                                           ident[:, :])
                ins.then_inc(s_y, 1)

            def expert(e, par):
                if there(e, E):
                    first_layer(e, par)
                if there(e - 1, E):
                    out_turn(e - 1, 1 - par)
                if there(e, E):
                    second_layer(e, par, 0)
                if there(e + 1, E):
                    in_turn(e + 1, 1 - par)
                if there(e, E):
                    second_layer(e, par, 1)

            sweep(pe, expert, 1, 1, E)


_INS = ["x", "adj", "L0_gnn_W", "L0_gnn_a1", "L0_gnn_a2", "L0_ffn_Wr", "L0_ffn_br", "L0_ffn_W1",
        "L0_ffn_b1", "L0_ffn_W2", "L0_ffn_b2"]


def kernel(**inputs):
    import numpy as _np
    import concourse.bacc as _bacc
    from concourse import mybir as _mybir
    from concourse.bass_utils import run_bass_kernel_spmd as _run

    nc = _bacc.Bacc("TRN2", target_bir_lowering=False, num_devices=1)
    arrays, args = {}, []
    for name in _INS:
        a = _np.ascontiguousarray(inputs[name])
        arrays[f"in_{name}_dram"] = a
        args.append(nc.dram_tensor(f"in_{name}_dram", a.shape, _mybir.dt.from_np(a.dtype), kind="ExternalInput").ap())
    shape = inputs["x"].shape
    args.append(nc.dram_tensor("out_0_dram", shape, _mybir.dt.float32, kind="ExternalOutput").ap())
    gat_moe(nc, *args)
    r = _run(nc, [arrays], core_ids=[0])
    return r.results[0]["out_0_dram"]
```

```python
from contextlib import ExitStack

import concourse.bass as bass
from concourse import mybir

ALU = mybir.AluOpType
ACT = mybir.ActivationFunctionType
AX = mybir.AxisListType
F32 = mybir.dt.float32
F32R = mybir.dt.float32r
BF16 = mybir.dt.bfloat16
I32 = mybir.dt.int32
U32 = mybir.dt.uint32

P = 128
MASKED = -9e15
SLOPE = 0.2
EPS = 1e-5
LEAST = -3.0e38


def gat_moe(nc, x, adj, W, a1, a2, Wr, br, W1, b1, W2, b2, out):
    N, D = x.shape
    E = Wr.shape[1]
    KC = D // P
    NT = (N + P - 1) // P
    TAIL = N - (NT - 1) * P
    CAP = N // E - 1
    CAP2 = CAP - P
    SLOTS = E * CAP
    ROW = D + 2
    NOWHERE = 5000
    H0 = D // 2
    WC = D + 2
    BANKS3 = (0, 4, 8, NT)
    assert D == 512 and E == 8 and P < CAP <= 2 * P and NT == 11 and TAIL < P

    x1_d = nc.dram_tensor("x1_rows", [N, D], F32).ap()
    disp = nc.dram_tensor("dispatched", [SLOTS + N, ROW], F32).ap()

    def rows(t):
        return TAIL if isinstance(t, int) and t == NT - 1 else P

    def there(t, n=NT):
        return not isinstance(t, int) or 0 <= t < n

    with ExitStack() as ctx:
        def sb(name, shape, dt=F32):
            return ctx.enter_context(nc.sbuf_tensor(name, shape, dt))

        def sem(name):
            return ctx.enter_context(nc.semaphore(name))

        x_all = sb("x_all", [P, NT, D])
        h_hi = sb("h_hi", [P, NT, D], F32R)
        h_lo = sb("h_lo", [P, NT, D], F32R)
        w_raw = sb("w_raw", [P, KC, D])
        w_hi = sb("w_hi", [P, KC, WC], F32R)
        w_lo = sb("w_lo", [P, KC, WC], F32R)
        xn = sb("xn", [P, 2, D])
        xt_hi = sb("xt_hi", [P, 2, KC, P], F32R)
        xt_lo = sb("xt_lo", [P, 2, KC, P], F32R)
        f2b = sb("f2b", [P, N])
        adj_s = sb("adj_s", [P, 2, N], I32)
        score = sb("score", [P, N])
        score2 = sb("score2", [P, N])
        prob = sb("prob", [P, 2, N])
        pt_hi = sb("pt_hi", [P, 2, NT, P], F32R)
        pt_lo = sb("pt_lo", [P, 2, NT, P], F32R)
        w1_s = sb("w1_s", [P, 2, KC, D])
        w2_s = sb("w2_s", [P, 2, KC, D])
        ident = sb("ident", [P, P])
        upto = sb("upto", [P, P], BF16)
        ones = sb("ones", [P, P], BF16)
        vecs = sb("vecs", [P, 4, D])
        a2_b, wa2_b = vecs[:, 0, :], vecs[:, 2, :]
        one_row = sb("one_row", [1, P])
        wa = sb("wa", [P, 2, KC])
        wr_s = sb("wr_s", [P, KC, E])
        br_b = sb("br_b", [P, E])
        b_cols = sb("b_cols", [P, 2, E * KC])
        half = sb("half", [P, 1])
        iota_e = sb("iota_e", [P, E])
        token1 = sb("token1", [P, NT])
        dump1 = sb("dump1", [P, NT])
        stat = sb("stat", [P, 6])
        mv = sb("mv", [P, 2, 2])
        ve = sb("ve", [P, 2, 1])
        rstd = sb("rstd", [P, 2, 1])
        stat2 = sb("stat2", [P, 6])
        mv2 = sb("mv2", [P, 2])
        ve2 = sb("ve2", [P, 1])
        rstd2 = sb("rstd2", [P, 1])
        f1 = sb("f1", [P, NT])
        f2 = sb("f2", [P, NT])
        fmax = sb("fmax", [P, 1])
        zmax = sb("zmax", [P, 1])
        rmax = sb("rmax", [P, 1])
        off_a = sb("off_a", [P, 1])
        off_b = sb("off_b", [P, 1])
        rsum = sb("rsum", [P, 2, 1])
        rinv = sb("rinv", [P, 2, 1])
        logit = sb("logit", [P, E])
        nmax = sb("nmax", [P, 1])
        pe8 = sb("pe8", [P, E])
        zsum = sb("zsum", [P, 1])
        top8 = sb("top8", [P, E])
        idx8 = sb("idx8", [P, E], U32)
        zinv = sb("zinv", [P, 1])
        idxf = sb("idxf", [P, 2, 1])
        onehot = sb("onehot", [P, 2, E], BF16)
        counts = sb("counts", [P, E], BF16)
        junk8 = sb("junk8", [P, E])
        pos = sb("pos", [P, 2, 1])
        fits = sb("fits", [P, 1])
        place = sb("place", [P, 1])
        place_d = sb("place_d", [P, 1])
        slot_f = sb("slot_f", [P, 1])
        slot_g = sb("slot_g", [P, 1])
        slot = sb("slot", [P, 2, 1], U32)
        relu_s = w_raw[:, 0, :]
        xn2 = w_raw[:, 2:4, :]
        b_rows = w_raw[0:E * KC, 1, 0:2 * P].rearrange("q (j p) -> q j p", j=2)
        row_s = vecs[:, :, :].rearrange("p i n -> p (i n)")[:, 0:2 * ROW].rearrange("p (i n) -> p i n", i=2)
        x2t = xn[:, :, :].rearrange("p i (c n) -> p i c n", c=KC)
        zeros = score2[:, 0:ROW]
        w_dot = prob[:, :, :].rearrange("p i n -> p (i n)")[:, 0:KC * D].rearrange("p (c n) -> p c n", c=KC)
        dot = score[:, 0:2 * D].rearrange("p (i n) -> p i n", i=2)
        junks = (vecs[:, 2, :], vecs[:, 3, :], dot[:, 0, :], dot[:, 1, :])
        a_rows = vecs[0:1, 1, :], f2b[0:1, 0:D]
        disp_s = score[:, 0:2 * ROW].rearrange("p (j n) -> p j n", j=2)
        disp_o = score2[:, 0:2 * ROW].rearrange("p (j n) -> p j n", j=2)
        dispatched = (disp_s, disp_o)
        gx_t = [prob[:, i, 0:KC * CAP].rearrange("p (c n) -> p c n", c=KC) for i in range(2)]
        hid = [adj_s[:, i, 0:KC * CAP].bitcast(F32).rearrange("p (c n) -> p c n", c=KC) for i in range(2)]
        eo_t = [adj_s[:, i, KC * CAP:2 * KC * CAP].bitcast(F32).rearrange("p (c n) -> p c n", c=KC)
                for i in range(2)]
        x1_g = w_raw[:, :, :].rearrange("p (i j) n -> p i j n", i=2)
        fin = vecs[:, :, :].rearrange("p (i j) n -> p i j n", i=2)
        gate_s = sb("gate_s", [P, 2, 2])
        emp = sb("emp", [P, 2])
        tokf = sb("tokf", [P, 2])
        dest = sb("dest", [P, 2, 2], U32)
        src = sb("src", [P, 2, 2], U32)

        banks = [ctx.enter_context(nc.psum_tensor(f"bank{i}", [P, 512], F32)) for i in range(8)]
        xt_ps = (banks[0], banks[1])
        h_ps = ((banks[2], banks[3]), (banks[4], banks[5]))
        row_ps, b_ps, a_ps = (banks[6], banks[7], banks[1]), banks[0], (banks[4], banks[5])
        pt_ps = (banks[1], banks[2], banks[3])
        o_ps = (banks[4], banks[5])
        x2_ps, logit_ps, pos_ps = banks[6], banks[7], banks[0]
        gx_ps, hid_ps, eo_ps, y_ps = ((banks[0], banks[1]), (banks[2], banks[3]),
                                      (banks[4], banks[5]), (banks[6], banks[7]))

        s_x = [sem("s_x_even"), sem("s_x_odd")]
        s_w, s_a, s_small, s_bias = sem("s_w"), sem("s_a"), sem("s_small"), sem("s_bias")
        s_adj = [sem("s_adj0"), sem("s_adj1")]
        s_zero = sem("s_zero")
        s_w1 = [sem("s_w1_0"), sem("s_w1_1")]
        s_w2 = [sem("s_w2_0"), sem("s_w2_1")]
        s_const, s_fill, s_held = sem("s_const"), sem("s_fill"), sem("s_held")
        s_stat, s_mv, s_ve, s_rstd, s_xn = (sem(n) for n in ("s_stat", "s_mv", "s_ve", "s_rstd", "s_xn"))
        s_ab, s_a2b, s_wdot, s_wsum, s_dot = (sem(n) for n in ("s_ab", "s_a2b", "s_wdot", "s_wsum", "s_dot"))
        s_f2, s_xt, s_xhi, s_xlo = (sem(n) for n in ("s_f2", "s_xt", "s_xhi", "s_xlo"))
        s_h, s_hhi, s_hlo = (sem(n) for n in ("s_h", "s_hhi", "s_hlo"))
        s_wa, s_whi, s_wa1, s_wlo, s_wa2t, s_wa2b = (
            sem(n) for n in ("s_wa", "s_whi", "s_wa1", "s_wlo", "s_wa2t", "s_wa2b"))
        s_row, s_f2b, s_bt, s_bc = (sem(n) for n in ("s_row", "s_f2b", "s_bt", "s_bc"))
        s_pen, s_fmax, s_zmax, s_rmax, s_off = (
            sem(n) for n in ("s_pen", "s_fmax", "s_zmax", "s_rmax", "s_off"))
        s_low, s_arg, s_prob, s_rinv = (sem(n) for n in ("s_low", "s_arg", "s_prob", "s_rinv"))
        s_pt = [sem(f"s_pt{b}") for b in range(3)]
        s_phi = [sem(f"s_phi{b}") for b in range(3)]
        s_plo = [sem(f"s_plo{b}") for b in range(3)]
        s_o, s_relu, s_x1 = sem("s_o"), sem("s_relu"), sem("s_x1")
        s_out = [sem("s_out0"), sem("s_out1")]
        s_stat2, s_mv2, s_ve2, s_rstd2, s_xn2 = (
            sem(n) for n in ("s_stat2", "s_mv2", "s_ve2", "s_rstd2", "s_xn2"))
        s_x2t, s_x2, s_logit = sem("s_x2t"), sem("s_x2"), sem("s_logit")
        s_lg, s_nmax, s_pe8, s_top, s_idx, s_idxf, s_onehot = (
            sem(n) for n in ("s_lg", "s_nmax", "s_pe8", "s_top", "s_idx", "s_idxf", "s_onehot"))
        s_zinv, s_gate, s_gx = sem("s_zinv"), sem("s_gate"), sem("s_gx")
        s_post, s_count, s_pos, s_fits, s_place, s_dist, s_slotf, s_slotg, s_slot = (
            sem(n) for n in ("s_post", "s_count", "s_pos", "s_fits", "s_place", "s_dist", "s_slotf", "s_slotg", "s_slot"))
        s_scat = [sem("s_scat0"), sem("s_scat1")]
        s_in = [sem("s_in0"), sem("s_in1")]
        s_gt, s_gxt, s_hidv, s_eol, s_eov = (sem(n) for n in ("s_gt", "s_gxt", "s_hidv", "s_eol", "s_eov"))
        s_hid, s_eo, s_y, s_fin = (sem(n) for n in ("s_hid", "s_eo", "s_y", "s_fin"))
        s_emp, s_tok, s_dest = sem("s_emp"), sem("s_tok"), sem("s_dest")
        s_x1g = [sem("s_x1g0"), sem("s_x1g1")]
        s_end = [sem("s_end0"), sem("s_end1")]

        def landed(t, par, each=16):
            return (t - par) * (each // 2) + each

        def after(eng, sem_, t, lag):
            if not isinstance(t, int) or t >= lag:
                eng.wait_ge(sem_, t - (lag - 1))

        def after_halves(eng, sem_, e, lag):
            if not isinstance(e, int) or e >= lag:
                eng.wait_ge(sem_, e * 2 - 2 * (lag - 1))

        def hold(eng, sem_, value):
            eng.wait_ge(sem_, value)
            eng.sem_inc(s_held, 1)

        def sweep(eng, step, lag, ahead, n, first=2, start=None):
            last = (n - 1 - ahead) // 2 * 2
            for i in range(-ahead if start is None else start, first):
                step(i, i % 2)
            with eng.Fori(first // 2, last // 2) as pair:
                step(pair * 2, 0)
                step(pair * 2 + 1, 1)
            for i in range(last, n + lag):
                step(i, i % 2)

        block = ctx.enter_context(nc.Block())

        @block.sync
        def _(sp):
            def load_x(t, par):
                if not there(t):
                    return
                R = rows(t)
                if not isinstance(t, int) or t >= 2:
                    hold(sp, s_x[par], landed(t, par) - 16)
                if isinstance(t, int):
                    sp.dma_start(x_all[0:R, t, :], x[t * P:t * P + R, :]).then_inc(s_x[par], 16)
                else:
                    sp.dma_start(x_all[:, t, :], x[bass.ds(t * P, P), :]).then_inc(s_x[par], 16)

            load_x(0, 0)
            for row, a in zip(a_rows, (a1, a2)):
                sp.dma_start(row, a.rearrange("n o -> o n")).then_inc(s_a, 16)
            sweep(sp, load_x, 0, 0, NT, start=1)
            sp.dma_start(wr_s[:, :, :], Wr.rearrange("(c p) e -> p c e", p=P)).then_inc(s_small, 16)
            sp.dma_start(br_b[:, :], br.partition_broadcast(P)).then_inc(s_small, 16)

            def load_adj(t, par):
                if not there(t):
                    return
                R = rows(t)
                after(sp, s_fmax, t, 2)
                if isinstance(t, int):
                    sp.dma_start(adj_s[0:R, par, :], adj[t * P:t * P + R, :]).then_inc(s_adj[par], 16)
                else:
                    sp.dma_start(adj_s[:, par, :], adj[bass.ds(t * P, P), :]).then_inc(s_adj[par], 16)

            def store_x1(t, par):
                if not there(t):
                    return
                R = rows(t)
                hold(sp, s_x1, t + 1)
                if not isinstance(t, int) or t >= 2:
                    hold(sp, s_out[par], landed(t, par, 32) - 32)
                for d in (out, x1_d):
                    sp.dma_start(d[bass.ds(t * P, R), :], x_all[0:R, t, :]).then_inc(s_out[par], 16)

            def load_rows(e, par):
                after(sp, s_gt, e, 2)
                after(sp, s_tok, e, 2)
                base = e * CAP
                d = dispatched[par]
                sp.dma_start(d[:, 0, :], disp[bass.ds(base, P), :]).then_inc(s_in[par], 16)
                sp.dma_start(d[0:CAP2, 1, :], disp[bass.ds(base + P, CAP2), :]).then_inc(s_in[par], 16)

            def load_expert(e, par):
                if isinstance(e, int):
                    v1, v2 = W1[e, :, :], W2[e, :, :]
                else:
                    v1 = W1[bass.ds(e, 1), :, :].rearrange("a k n -> (a k) n")
                    v2 = W2[bass.ds(e, 1), :, :].rearrange("a k n -> (a k) n")
                after_halves(sp, s_hid, e, 2)
                sp.dma_start(w1_s[:, par, :, :], v1.rearrange("(c p) n -> p c n", p=P)).then_inc(s_w1[par], 16)
                if not isinstance(e, int) or e >= 2:
                    load_rows(e, par)
                after_halves(sp, s_eo, e, 2)
                sp.dma_start(w2_s[:, par, :, :], v2.rearrange("(c p) n -> p c n", p=P)).then_inc(s_w2[par], 16)

            load_adj(0, 0)
            load_adj(1, 1)
            sp.wait_ge(s_fill, 3)
            ZP = SLOTS // 12
            sp.dma_start(disp[0:SLOTS, :].rearrange("(p j) n -> p j n", p=ZP),
                         zeros[0:ZP, :].unsqueeze(1).broadcast_to([ZP, 12, ROW])).then_inc(s_zero, 16)

            def tile(t, par):
                if there(t + 2) and not (isinstance(t, int) and t < 0):
                    load_adj(t + 2, par)
                store_x1(t - 1, 1 - par)

            for t in range(0, 2):
                tile(t, t % 2)
            load_expert(0, 0)
            load_expert(1, 1)
            with sp.Fori(1, 8 // 2) as pair:
                t = pair * 2
                tile(t, 0)
                tile(t + 1, 1)
            for t in range(8, NT + 1):
                tile(t, t % 2)

            sp.wait_ge(s_scat[0], landed(10, 0))
            sp.wait_ge(s_scat[1], landed(9, 1))
            load_rows(0, 0)
            load_rows(1, 1)
            sweep(sp, load_expert, 0, 0, E, start=2)
            sp.wait_ge(s_end[0], 32 * (E // 2))
            sp.wait_ge(s_end[1], 32 * (E // 2))

        @block.gpsimd
        def _(pool):
            pool.memset(ident[:, :], 0.0).then_inc(s_fill, 1)
            pool.memset(upto[:, :], 1.0).then_inc(s_fill, 1)
            pool.memset(zeros[:, :], 0.0).then_inc(s_fill, 1)
            pool.memset(one_row[:, :], 1.0).then_inc(s_fill, 1)
            pool.memset(half[:, :], -0.5).then_inc(s_const, 1)
            pool.wait_ge(s_fill, 2)
            pool.affine_select(out=ident[:, :], in_=ident[:, :], compare_op=ALU.not_equal, fill=1.0,
                               base=0, pattern=[[-1, P]], channel_multiplier=1).then_inc(s_const, 1)
            pool.affine_select(out=upto[:, :], in_=upto[:, :], compare_op=ALU.is_ge, fill=0.0,
                               base=0, pattern=[[1, P]], channel_multiplier=-1).then_inc(s_const, 1)
            pool.memset(w_hi[:, :, H0 + 1:H0 + 2].bitcast(F32), 0.0).then_inc(s_const, 1)
            pool.memset(w_lo[:, :, H0 + 1:H0 + 2].bitcast(F32), 0.0).then_inc(s_const, 1)
            pool.memset(ones[:, :], 1.0).then_inc(s_const, 1)
            pool.memset(counts[:, :], 0.0).then_inc(s_const, 1)
            pool.iota(iota_e[:, :], pattern=[[1, E]], base=0, channel_multiplier=0,
                      allow_small_or_imprecise_dtypes=True).then_inc(s_const, 1)
            pool.iota(token1[:, :], pattern=[[P, NT]], base=1, channel_multiplier=1,
                      allow_small_or_imprecise_dtypes=True).then_inc(s_const, 1)
            pool.iota(dump1[:, :], pattern=[[P, NT]], base=SLOTS + 1, channel_multiplier=1,
                      allow_small_or_imprecise_dtypes=True).then_inc(s_const, 1)
            pool.wait_ge(s_const, 1)

            def power(t, par):
                if not there(t):
                    return
                R = rows(t)
                pool.wait_ge(s_ve, t + 1)
                after(pool, s_xn, t, 2)
                pool.tensor_tensor(rstd[0:R, par, :], ve[0:R, par, :], half[0:R, :], ALU.pow).then_inc(s_rstd, 1)

            def f2_product(t, par):
                R = rows(t)
                pool.wait_ge(s_xn, t + 1)
                if isinstance(t, int) and t == 0:
                    pool.wait_ge(s_wa2b, 1)
                after(pool, s_f2, t, 2)
                pool.tensor_tensor(dot[0:R, par, :], xn[0:R, par, :], wa2_b[0:R, :], ALU.mult).then_inc(s_dot, 1)

            def tile1(t, par):
                if there(t + 1) and not (isinstance(t, int) and t == -1):
                    f2_product(t + 1, 1 - par)
                if there(t + 2):
                    power(t + 2, par)
                if isinstance(t, int) and t == -1:
                    f2_product(0, 0)
                if isinstance(t, int) and t == -2:
                    pool.wait_ge(s_a2b, 1)
                    pool.wait_ge(s_w, 16)
                    for c in range(KC):
                        pool.tensor_tensor(w_dot[:, c, :], w_raw[:, c, :], a2_b[:, :], ALU.mult).then_inc(s_wdot, 1)

            sweep(pool, tile1, -1, 2, NT)

            def residual(t, par):
                R = rows(t)
                pool.wait_ge(s_relu, t + 1)
                pool.tensor_tensor(x_all[0:R, t, :], x_all[0:R, t, :], relu_s[0:R, :], ALU.add).then_inc(s_x1, 1)

            def power2(t, par):
                R = rows(t)
                pool.wait_ge(s_ve2, t + 1)
                pool.tensor_tensor(rstd2[0:R, :], ve2[0:R, :], half[0:R, :], ALU.pow).then_inc(s_rstd2, 1)

            def place_rows(t, par):
                R = rows(t)
                hold(pool, s_pos, t + 1)
                pool.tensor_scalar(fits[0:R, :], pos[0:R, par, :], float(CAP), None, ALU.is_le).then_inc(s_fits, 1)
                pool.tensor_scalar(place[0:R, :], idxf[0:R, par, :], float(CAP), pos[0:R, par, :], ALU.mult,
                                   ALU.add).then_inc(s_place, 1)
                dump = dump1[0:R, bass.ds(t, 1)]
                hold(pool, s_place, t + 1)
                pool.tensor_tensor(place_d[0:R, :], place[0:R, :], dump, ALU.subtract).then_inc(s_dist, 1)
                hold(pool, s_dist, t + 1)
                pool.tensor_tensor(slot_f[0:R, :], place_d[0:R, :], fits[0:R, :], ALU.mult).then_inc(s_slotf, 1)
                hold(pool, s_slotf, t + 1)
                pool.tensor_tensor(slot_g[0:R, :], slot_f[0:R, :], dump, ALU.add).then_inc(s_slotg, 1)
                hold(pool, s_slotg, t + 1)
                if not isinstance(t, int) or t >= 2:
                    hold(pool, s_scat[par], landed(t, par) - 16)
                pool.tensor_scalar(slot[0:R, par, :], slot_g[0:R, :], -1.0, None, ALU.add).then_inc(s_slot, 1)

            def scatter(t, par):
                R = rows(t)
                pool.wait_ge(s_gx, t + 1)
                hold(pool, s_slot, t + 1)
                pool.indirect_dma_start(disp, bass.IndirectOffsetOnAxis(ap=slot[0:R, par, :], axis=0),
                                        row_s[0:R, par, :], None).then_inc(s_scat[par], 16)

            def tile(t, par):
                if there(t - 1):
                    residual(t - 1, 1 - par)
                    power2(t - 1, 1 - par)
                if there(t - 3):
                    place_rows(t - 3, 1 - par)
                    scatter(t - 3, 1 - par)

            pool.wait_ge(s_zero, 16)
            pool.wait_ge(s_const, 10)
            sweep(pool, tile, 3, 2, NT, first=4, start=1)

            def gather_x1(e, par):
                hold(pool, s_dest, e + 1)
                for j, R in ((0, P), (1, CAP2)):
                    pool.indirect_dma_start(x1_g[0:R, par, j, :], None, x1_d,
                                            bass.IndirectOffsetOnAxis(ap=src[0:R, par, j:j + 1], axis=0)
                                            ).then_inc(s_x1g[par], 16)

            def scatter_out(e, par):
                for j, R in ((0, P), (1, CAP2)):
                    hold(pool, s_fin, e * 2 + j + 1)
                    pool.indirect_dma_start(out, bass.IndirectOffsetOnAxis(ap=dest[0:R, par, j:j + 1], axis=0),
                                            fin[0:R, par, j, :], None, bounds_check=N - 1, oob_is_err=False
                                            ).then_inc(s_end[par], 16)

            pool.wait_ge(s_out[0], landed(10, 0, 32))
            pool.wait_ge(s_out[1], landed(9, 1, 32))

            def expert(e, par):
                if there(e - 1, E):
                    scatter_out(e - 1, 1 - par)
                if there(e + 1, E):
                    gather_x1(e + 1, 1 - par)

            sweep(pool, expert, 1, 1, E)

        @block.scalar
        def _(act):
            act.dma_start(w_raw[:, :, :], W.rearrange("(c p) n -> p c n", p=P)).then_inc(s_w, 16)

            def x_high(t, par):
                R = rows(t)
                act.wait_ge(s_xt, t + 1)
                after(act, s_h, t, 2)
                src_ = xt_ps[par][:, :].rearrange("p (c n) -> p c n", c=KC)
                act.activation(xt_hi[:, par, :, 0:R], src_[:, :, 0:R], ACT.Copy).then_inc(s_xhi, 1)

            def h_high(t, par):
                R = rows(t)
                act.wait_ge(s_h, t + 1)
                for j in range(2):
                    ins = act.activation(h_hi[0:R, t, j * H0:(j + 1) * H0], h_ps[par][j][0:R, 0:H0], ACT.Copy)
                ins.then_inc(s_hhi, 1)

            def f2_sum(t, par):
                R = rows(t)
                act.wait_ge(s_dot, t + 1)
                act.activation(dot[0:R, par, :], dot[0:R, par, :], ACT.Copy,
                               accum_out=f2[0:R, bass.ds(t, 1)]).then_inc(s_f2, 1)

            def weights1():
                act.wait_ge(s_w, 16)
                act.activation(w_hi[:, :, H0 + 2:WC], w_raw[:, :, H0:D], ACT.Copy).then_inc(s_whi, 1)
                act.activation(w_hi[:, :, 0:H0], w_raw[:, :, 0:H0], ACT.Copy).then_inc(s_whi, 1)
                act.wait_ge(s_ab, 2)
                act.activation(a2_b[:, :], a_ps[1][:, :], ACT.Copy).then_inc(s_a2b, 1)
                act.wait_ge(s_wa, KC)
                act.activation(w_hi[:, :, H0], wa[:, 0, :], ACT.Copy).then_inc(s_wa1, 1)
                for c in range(KC):
                    act.wait_ge(s_wdot, c + 1)
                    act.activation(w_dot[:, c, :], w_dot[:, c, :], ACT.Copy,
                                   accum_out=wa[:, 1, c:c + 1]).then_inc(s_wsum, 1)
                act.wait_ge(s_wa2t, 1)
                act.activation(wa2_b[:, :], row_ps[0][:, :], ACT.Copy).then_inc(s_wa2b, 1)

            def tile1(t, par):
                if there(t + 1):
                    x_high(t + 1, 1 - par)
                if there(t - 1):
                    h_high(t - 1, 1 - par)
                if isinstance(t, int) and t == -1:
                    weights1()
                if there(t + 1):
                    f2_sum(t + 1, 1 - par)

            sweep(act, tile1, -1, 1, NT)

            act.wait_ge(s_wlo, 3)
            act.dma_start(b_rows[:, 0, :], b1.rearrange("e (c p) -> (e c) p", p=P)).then_inc(s_bias, 16)
            act.dma_start(b_rows[:, 1, :], b2.rearrange("e (c p) -> (e c) p", p=P)).then_inc(s_bias, 16)
            for b in range(3):
                lo, hi = BANKS3[b] * P, min(BANKS3[b + 1] * P, N)
                act.wait_ge(s_row, b + 1)
                act.activation(f2b[:, lo:hi], row_ps[b][:, 0:hi - lo], ACT.Copy).then_inc(s_f2b, 1)

            def relu_out(t, par):
                R = rows(t)
                act.wait_ge(s_o, t + 1)
                act.wait_ge(s_rinv, t + 1)
                after(act, s_x1, t, 1)
                act.activation(relu_s[0:R, :], o_ps[par][0:R, :], ACT.Relu, scale=rinv[0:R, par, :]
                               ).then_inc(s_relu, 1)

            def p_high(t, par, b):
                R = rows(t)
                act.wait_ge(s_pt[b], t + 1)
                after(act, s_o, t, 2)
                k0, k1 = BANKS3[b], BANKS3[b + 1]
                v = pt_ps[b][:, 0:(k1 - k0) * P].rearrange("p (k n) -> p k n", n=P)
                if b < 2:
                    act.activation(pt_hi[:, par, k0:k1, 0:R], v[:, :, 0:R], ACT.Copy).then_inc(s_phi[b], 1)
                else:
                    act.activation(pt_hi[:, par, k0:k1 - 1, 0:R], v[:, 0:k1 - k0 - 1, 0:R], ACT.Copy)
                    act.activation(pt_hi[0:TAIL, par, k1 - 1, 0:R], v[0:TAIL, k1 - k0 - 1, 0:R], ACT.Copy
                                   ).then_inc(s_phi[b], 1)

            def low_slope(t, par):
                R = rows(t)
                act.wait_ge(s_off, 2 * (t + 1))
                act.activation(score2[0:R, :], score[0:R, :], ACT.Identity, scale=SLOPE, bias=off_b[0:R, :]
                               ).then_inc(s_low, 1)

            def exps(t, par):
                R = rows(t)
                act.wait_ge(s_arg, t + 1)
                after(act, s_pt[2], t, 2)
                after(act, s_rinv, t, 2)
                act.activation(prob[0:R, par, :], score[0:R, :], ACT.Exp,
                               accum_out=rsum[0:R, par, :]).then_inc(s_prob, 1)

            def x2_copy(t, par):
                R = rows(t)
                act.wait_ge(s_x2t, t + 1)
                v = x2_ps[:, :].rearrange("p (c n) -> p c n", c=KC)
                act.activation(x2t[:, par, :, 0:R], v[:, :, 0:R], ACT.Copy).then_inc(s_x2, 1)

            def exp8(t, par):
                R = rows(t)
                act.wait_ge(s_nmax, t + 1)
                act.activation(pe8[0:R, :], logit[0:R, :], ACT.Exp, bias=nmax[0:R, :],
                               accum_out=zsum[0:R, :]).then_inc(s_pe8, 1)

            def gated(t, par):
                R = rows(t)
                act.wait_ge(s_gate, t + 1)
                act.activation(row_s[0:R, par, 0:D], xn2[0:R, par, :], ACT.Copy,
                               scale=row_s[0:R, par, D:D + 1]).then_inc(s_gx, 1)

            def tile2(t, par):
                if there(t - 1):
                    relu_out(t - 1, 1 - par)
                if there(t - 2):
                    x2_copy(t - 2, par)
                if there(t + 1):
                    p_high(t + 1, 1 - par, 0)
                    p_high(t + 1, 1 - par, 1)
                if there(t + 2):
                    low_slope(t + 2, par)
                if there(t - 2):
                    exp8(t - 2, par)
                if there(t + 2):
                    exps(t + 2, par)
                if there(t - 2):
                    gated(t - 2, par)
                if there(t + 1):
                    p_high(t + 1, 1 - par, 2)

            act.wait_ge(s_zero, 16)
            h_high(NT - 2, 1)
            low_slope(0, 0)
            h_high(NT - 1, 0)
            exps(0, 0)
            for b in range(3):
                p_high(0, 0, b)
            low_slope(1, 1)
            exps(1, 1)
            act.wait_ge(s_bt, 1)
            act.activation(b_cols[:, :, :], b_ps[:, 0:2 * E * KC].rearrange("p (j n) -> p j n", j=2),
                           ACT.Copy).then_inc(s_bc, 1)
            sweep(act, tile2, 2, 2, NT, first=4, start=0)

            def gx_copy(e, par):
                act.wait_ge(s_gt, e + 1)
                after_halves(act, s_hid, e, 2)
                for j in range(2):
                    ins = act.activation(gx_t[par][:, 2 * j:2 * j + 2, :],
                                         gx_ps[j][:, 0:2 * CAP].rearrange("p (c n) -> p c n", c=2), ACT.Copy)
                ins.then_inc(s_gxt, 1)

            def hid_relu(e, par):
                after_halves(act, s_eo, e, 2)
                for c in range(KC):
                    if c % 2 == 0:
                        act.wait_ge(s_hid, e * 2 + c // 2 + 1)
                    ins = act.activation(hid[par][:, c, :], hid_ps[c // 2][:, (c % 2) * CAP:(c % 2 + 1) * CAP],
                                         ACT.Relu, bias=b_cols[:, 0, bass.ds(e * KC + c, 1)])
                ins.then_inc(s_hidv, 1)

            def eo_bias_low(e, par):
                act.wait_ge(s_eo, e * 2 + 1)
                after_halves(act, s_y, e, 2)
                for c in range(KC // 2):
                    ins = act.activation(eo_t[par][:, c, :], eo_ps[0][:, c * CAP:(c + 1) * CAP],
                                         ACT.Identity, bias=b_cols[:, 1, bass.ds(e * KC + c, 1)])
                ins.then_inc(s_eol, 1)

            act.wait_ge(s_bc, 1)

            def expert(e, par):
                if there(e, E):
                    hid_relu(e, par)
                if there(e + 1, E):
                    gx_copy(e + 1, 1 - par)
                if there(e, E):
                    eo_bias_low(e, par)

            sweep(act, expert, 0, 1, E)

        @block.vector
        def _(dve):
            def stats(t, par):
                R = rows(t)
                dve.wait_ge(s_x[par], landed(t, par))
                dve.bn_stats(stat[0:R, :], x_all[0:R, t, :]).then_inc(s_stat, 1)

            def variance(t, par):
                R = rows(t)
                hold(dve, s_stat, t + 1)
                dve.bn_aggr(mv[0:R, par, :], stat[0:R, :]).then_inc(s_mv, 1)
                dve.wait_ge(s_mv, t + 1)
                after(dve, s_rstd, t, 2)
                dve.tensor_scalar(ve[0:R, par, :], mv[0:R, par, 1:2], EPS, None, ALU.add).then_inc(s_ve, 1)

            def normal(t, par):
                R = rows(t)
                dve.wait_ge(s_rstd, t + 1)
                after(dve, s_xt, t, 2)
                after(dve, s_dot, t, 2)
                dve.tensor_scalar(xn[0:R, par, :], x_all[0:R, t, :], mv[0:R, par, 0:1], rstd[0:R, par, :],
                                  ALU.subtract, ALU.mult).then_inc(s_xn, 1)

            def x_low(t, par):
                R = rows(t)
                dve.wait_ge(s_xhi, t + 1)
                v = xt_ps[par][:, :].rearrange("p (c n) -> p c n", c=KC)
                dve.tensor_tensor(xt_lo[:, par, :, 0:R], v[:, :, 0:R], xt_hi[:, par, :, 0:R].bitcast(F32),
                                  ALU.subtract).then_inc(s_xlo, 1)

            def h_low(t, par):
                R = rows(t)
                dve.wait_ge(s_hhi, t + 1)
                for j in range(2):
                    dve.tensor_tensor(h_lo[0:R, t, j * H0:(j + 1) * H0], h_ps[par][j][0:R, 0:H0],
                                      h_hi[0:R, t, j * H0:(j + 1) * H0].bitcast(F32), ALU.subtract)
                dve.tensor_copy(f1[0:R, bass.ds(t, 1)], h_ps[par][0][0:R, H0:H0 + 1]).then_inc(s_hlo, 1)

            def weights1():
                dve.wait_ge(s_ab, 1)
                dve.wait_ge(s_w, 16)
                for c in range(KC):
                    dve.tensor_tensor_reduce(junks[c], w_raw[:, c, :], a_ps[0][:, :], 1.0, 0.0, ALU.mult,
                                             ALU.add, wa[:, 0, c:c + 1]).then_inc(s_wa, 1)
                dve.wait_ge(s_whi, 1)
                dve.tensor_tensor(w_lo[:, :, H0 + 2:WC], w_raw[:, :, H0:D], w_hi[:, :, H0 + 2:WC].bitcast(F32),
                                  ALU.subtract).then_inc(s_wlo, 1)
                x_low(0, 0)
                dve.wait_ge(s_whi, 2)
                dve.tensor_tensor(w_lo[:, :, 0:H0], w_raw[:, :, 0:H0], w_hi[:, :, 0:H0].bitcast(F32),
                                  ALU.subtract).then_inc(s_wlo, 1)
                dve.wait_ge(s_wa1, 1)
                dve.tensor_tensor(w_lo[:, :, H0], wa[:, 0, :], w_hi[:, :, H0].bitcast(F32),
                                  ALU.subtract).then_inc(s_wlo, 1)

            def tile1(t, par):
                if there(t + 2):
                    stats(t + 2, par)
                    variance(t + 2, par)
                if there(t + 1) and not (isinstance(t, int) and t == -1):
                    x_low(t + 1, 1 - par)
                if there(t + 2):
                    normal(t + 2, par)
                if isinstance(t, int) and t == -2:
                    weights1()
                if there(t - 1):
                    h_low(t - 1, 1 - par)

            sweep(dve, tile1, -1, 2, NT)

            def penalty(t, par):
                R = rows(t)
                dve.wait_ge(s_adj[par], landed(t, par))
                dve.tensor_scalar(adj_s[0:R, par, :].bitcast(F32), adj_s[0:R, par, :], 0.0, MASKED,
                                  ALU.is_le, ALU.mult).then_inc(s_pen, 1)

            def scores(t, par):
                R = rows(t)
                pen = adj_s[0:R, par, :].bitcast(F32)
                after(dve, s_prob, t, 1)
                hold(dve, s_pen, t + 1)
                dve.tensor_tensor_reduce(score[0:R, :], pen, f2b[0:R, :], 1.0, LEAST, ALU.add, ALU.max,
                                         fmax[0:R, :]).then_inc(s_fmax, 1)

            def offsets(t, par):
                R = rows(t)
                f1t = f1[0:R, bass.ds(t, 1)]
                dve.wait_ge(s_fmax, t + 1)
                dve.tensor_tensor(zmax[0:R, :], fmax[0:R, :], f1t, ALU.add).then_inc(s_zmax, 1)
                dve.wait_ge(s_zmax, t + 1)
                dve.scalar_tensor_tensor(rmax[0:R, :], zmax[0:R, :], SLOPE, zmax[0:R, :], ALU.mult,
                                         ALU.max).then_inc(s_rmax, 1)
                dve.wait_ge(s_rmax, t + 1)
                dve.tensor_tensor(off_a[0:R, :], f1t, rmax[0:R, :], ALU.subtract).then_inc(s_off, 1)
                dve.scalar_tensor_tensor(off_b[0:R, :], f1t, SLOPE, rmax[0:R, :], ALU.mult,
                                         ALU.subtract).then_inc(s_off, 1)

            def argument(t, par):
                R = rows(t)
                dve.wait_ge(s_low, t + 1)
                dve.scalar_tensor_tensor(score[0:R, :], score[0:R, :], off_a[0:R, :], score2[0:R, :], ALU.add,
                                         ALU.max).then_inc(s_arg, 1)

            def sum_inverse(t, par):
                R = rows(t)
                dve.wait_ge(s_prob, t + 1)
                after(dve, s_relu, t, 2)
                dve.reciprocal(rinv[0:R, par, :], rsum[0:R, par, :]).then_inc(s_rinv, 1)

            def p_low(t, par, b):
                R = rows(t)
                dve.wait_ge(s_phi[b], t + 1)
                k0, k1 = BANKS3[b], BANKS3[b + 1]
                v = pt_ps[b][:, 0:(k1 - k0) * P].rearrange("p (k n) -> p k n", n=P)
                if b < 2:
                    dve.tensor_tensor(pt_lo[:, par, k0:k1, 0:R], v[:, :, 0:R],
                                      pt_hi[:, par, k0:k1, 0:R].bitcast(F32), ALU.subtract).then_inc(s_plo[b], 1)
                else:
                    dve.tensor_tensor(pt_lo[:, par, k0:k1 - 1, 0:R], v[:, 0:k1 - k0 - 1, 0:R],
                                      pt_hi[:, par, k0:k1 - 1, 0:R].bitcast(F32), ALU.subtract)
                    dve.tensor_tensor(pt_lo[0:TAIL, par, k1 - 1, 0:R], v[0:TAIL, k1 - k0 - 1, 0:R],
                                      pt_hi[0:TAIL, par, k1 - 1, 0:R].bitcast(F32), ALU.subtract
                                      ).then_inc(s_plo[b], 1)

            def stats2(t, par):
                R = rows(t)
                dve.wait_ge(s_x1, t + 1)
                dve.bn_stats(stat2[0:R, :], x_all[0:R, t, :]).then_inc(s_stat2, 1)

            def variance2(t, par):
                R = rows(t)
                hold(dve, s_stat2, t + 1)
                dve.bn_aggr(mv2[0:R, :], stat2[0:R, :]).then_inc(s_mv2, 1)
                dve.wait_ge(s_mv2, t + 1)
                dve.tensor_scalar(ve2[0:R, :], mv2[0:R, 1:2], EPS, None, ALU.add).then_inc(s_ve2, 1)

            def normal2(t, par):
                R = rows(t)
                dve.wait_ge(s_rstd2, t + 1)
                after(dve, s_gx, t, 2)
                dve.tensor_scalar(xn2[0:R, par, :], x_all[0:R, t, :], mv2[0:R, 0:1], rstd2[0:R, :],
                                  ALU.subtract, ALU.mult).then_inc(s_xn2, 1)

            def route(t, par):
                R = rows(t)
                dve.wait_ge(s_logit, t + 1)
                dve.tensor_tensor(logit[0:R, :], logit_ps[0:R, 0:E], br_b[0:R, :], ALU.add).then_inc(s_lg, 1)
                dve.wait_ge(s_lg, t + 1)
                dve.tensor_reduce(nmax[0:R, :], logit[0:R, :], AX.X, ALU.max, negate=True).then_inc(s_nmax, 1)

            def choose(t, par):
                R = rows(t)
                after(dve, s_place, t, 2)
                if not isinstance(t, int) or t >= 2:
                    hold(dve, s_scat[par], landed(t, par) - 16)
                hold(dve, s_pe8, t + 1)
                dve.max(top8[0:R, :], pe8[0:R, :]).then_inc(s_top, 1)
                dve.reciprocal(zinv[0:R, :], zsum[0:R, :]).then_inc(s_zinv, 1)
                hold(dve, s_top, t + 1)
                dve.max_index(idx8[0:R, :], top8[0:R, :], pe8[0:R, :]).then_inc(s_idx, 1)
                dve.wait_ge(s_zinv, t + 1)
                dve.tensor_tensor(row_s[0:R, par, D:D + 1], top8[0:R, 0:1], zinv[0:R, :], ALU.mult)
                dve.tensor_copy(row_s[0:R, par, D + 1:D + 2], token1[0:R, bass.ds(t, 1)]).then_inc(s_gate, 1)
                dve.wait_ge(s_idx, t + 1)
                dve.tensor_copy(idxf[0:R, par, :], idx8[0:R, 0:1]).then_inc(s_idxf, 1)
                dve.wait_ge(s_idxf, t + 1)
                dve.tensor_scalar(onehot[0:R, par, :], iota_e[0:R, :], idxf[0:R, par, :], None,
                                  ALU.is_equal).then_inc(s_onehot, 1)

            def positions(t, par):
                R = rows(t)
                dve.wait_ge(s_post, t + 1)
                after(dve, s_pos, t, 1)
                after(dve, s_place, t, 1)
                dve.tensor_tensor_reduce(junk8[0:R, :], pos_ps[0:R, 0:E], onehot[0:R, par, :], 1.0, 0.0,
                                         ALU.mult, ALU.add, pos[0:R, par, :]).then_inc(s_pos, 1)
                dve.tensor_tensor(counts[0:R, :], counts[0:R, :], onehot[0:R, par, :], ALU.add).then_inc(s_count, 1)

            def tile2(t, par):
                if isinstance(t, int) and t == 0:
                    penalty(2, 0)
                    scores(2, 0)
                    p_low(1, 1, 0)
                    offsets(2, 0)
                    p_low(1, 1, 1)
                    argument(2, 0)
                    sum_inverse(1, 1)
                    return
                if there(t):
                    p_low(t, par, 2)
                if there(t + 1):
                    p_low(t + 1, 1 - par, 0)
                if there(t + 1):
                    sum_inverse(t + 1, 1 - par)
                if there(t + 2):
                    penalty(t + 2, par)
                if isinstance(t, int) and there(t - 2) and not there(t):
                    route(t - 2, par)
                    choose(t - 2, par)
                if there(t - 1):
                    stats2(t - 1, 1 - par)
                if there(t + 2):
                    scores(t + 2, par)
                if there(t - 1):
                    variance2(t - 1, 1 - par)
                if there(t + 2):
                    offsets(t + 2, par)
                if there(t + 1):
                    p_low(t + 1, 1 - par, 1)
                if there(t - 1):
                    normal2(t - 1, 1 - par)
                if there(t - 2) and there(t):
                    route(t - 2, par)
                if there(t + 2):
                    argument(t + 2, par)
                if there(t - 3):
                    positions(t - 3, 1 - par)
                if there(t - 2) and there(t):
                    choose(t - 2, par)

            dve.wait_ge(s_const, 10)
            dve.wait_ge(s_small, 32)
            penalty(0, 0)
            dve.wait_ge(s_f2b, 3)
            scores(0, 0)
            offsets(0, 0)
            h_low(NT - 2, 1)
            argument(0, 0)
            h_low(NT - 1, 0)
            penalty(1, 1)
            scores(1, 1)
            p_low(0, 0, 0)
            offsets(1, 1)
            p_low(0, 0, 1)
            p_low(0, 0, 2)
            argument(1, 1)
            sum_inverse(0, 0)
            sweep(dve, tile2, 3, 2, NT, first=4, start=0)

            def tokens(e, par):
                dve.wait_ge(s_in[par], landed(e, par, 32))
                d = dispatched[par]
                if not isinstance(e, int) or e >= 2:
                    dve.wait_ge(s_end[par], landed(e, par, 32) - 32)
                after(dve, s_dest, e, 1)
                for j, R in ((0, P), (1, CAP2)):
                    dve.tensor_copy(gate_s[0:R, par, j:j + 1], d[0:R, j, D:D + 1])
                    ins = dve.tensor_scalar(emp[0:R, j:j + 1], d[0:R, j, D + 1:D + 2], 1.0, float(NOWHERE),
                                            ALU.is_lt, ALU.mult)
                    dve.tensor_scalar(tokf[0:R, j:j + 1], d[0:R, j, D + 1:D + 2], 1.0, -1.0,
                                      ALU.max, ALU.add)
                    ins = dve.tensor_scalar(src[0:R, par, j:j + 1], d[0:R, j, D + 1:D + 2], 1.0, -1.0,
                                            ALU.max, ALU.add)
                ins.then_inc(s_tok, 1)
                dve.wait_ge(s_tok, e + 1)
                for j, R in ((0, P), (1, CAP2)):
                    ins = dve.tensor_tensor(dest[0:R, par, j:j + 1], emp[0:R, j:j + 1], tokf[0:R, j:j + 1], ALU.add)
                ins.then_inc(s_dest, 1)

            def eo_bias_high(e, par):
                dve.wait_ge(s_eo, e * 2 + 2)
                after_halves(dve, s_y, e, 2)
                for c in range(KC // 2, KC):
                    ins = dve.tensor_scalar(eo_t[par][:, c, :], eo_ps[1][:, (c % 2) * CAP:(c % 2 + 1) * CAP],
                                            b_cols[:, 1, bass.ds(e * KC + c, 1)], None, ALU.add)
                ins.then_inc(s_eov, 1)

            def final(e, par):
                dve.wait_ge(s_x1g[par], landed(e, par, 32))
                for j, R in ((0, P), (1, CAP2)):
                    dve.wait_ge(s_y, e * 2 + j + 1)
                    dve.scalar_tensor_tensor(fin[0:R, par, j, :], y_ps[j][0:R, :], gate_s[0:R, par, j:j + 1],
                                             x1_g[0:R, par, j, :], ALU.mult, ALU.add).then_inc(s_fin, 1)

            def expert(e, par):
                if there(e - 1, E):
                    final(e - 1, 1 - par)
                if there(e, E):
                    eo_bias_high(e, par)
                if there(e + 1, E):
                    tokens(e + 1, 1 - par)

            dve.wait_ge(s_bc, 1)
            sweep(dve, expert, 1, 1, E)

        @block.tensor
        def _(pe):
            pe.wait_ge(s_const, 2)

            def x_turn(t, par):
                R = rows(t)
                pe.wait_ge(s_xn, t + 1)
                after(pe, s_xlo, t, 2)
                for c in range(KC):
                    ins = pe.transpose(xt_ps[par][:, c * P:c * P + R], xn[0:R, par, c * P:(c + 1) * P],
                                       ident[0:R, 0:R])
                ins.then_inc(s_xt, 1)

            def a_bcast():
                pe.wait_ge(s_fill, 4)
                pe.wait_ge(s_a, 32)
                for j in range(2):
                    pe.matmul(a_ps[j][:, :], one_row[:, :], a_rows[j], start=True, stop=True).then_inc(s_ab, 1)

            def h_product(t, par):
                R = rows(t)
                pe.wait_ge(s_xlo, t + 1)
                after(pe, s_hlo, t, 2)
                parts = ((xt_lo, w_hi), (xt_hi, w_lo), (xt_hi, w_hi))
                for j, (c0, c1) in ((1, (H0 + 2, WC)), (0, (0, H0 + 2))):
                    if isinstance(t, int) and t == 0:
                        pe.wait_ge(s_wlo, 1 if j == 1 else 3)
                    for n, (a, w) in enumerate(parts):
                        for c in range(KC):
                            ins = pe.matmul(h_ps[par][j][0:R, 0:c1 - c0], a[:, par, c, 0:R], w[:, c, c0:c1],
                                            start=(n == 0 and c == 0), stop=(n == 2 and c == KC - 1))
                ins.then_inc(s_h, 1)

            def f2_turn():
                pe.wait_ge(s_f2, NT)
                pe.wait_ge(s_wa2b, 1)
                pe.wait_ge(s_xlo, NT - 1)
                for b in range(3):
                    for t in range(BANKS3[b], BANKS3[b + 1]):
                        R = rows(t)
                        o = (t - BANKS3[b]) * P
                        ins = pe.matmul(row_ps[b][:, o:o + R], f2[0:R, t:t + 1].broadcast_to([R, P]),
                                        ident[0:R, 0:R], start=True, stop=True)
                    ins.then_inc(s_row, 1)

            def tile1(t, par):
                if there(t + 1):
                    x_turn(t + 1, 1 - par)
                if isinstance(t, int) and t == NT - 2:
                    f2_turn()
                if there(t):
                    h_product(t, par)
                if isinstance(t, int) and t == 0:
                    pe.wait_ge(s_wsum, KC)
                    for c in range(KC):
                        ins = pe.matmul(row_ps[0][:, c * P:(c + 1) * P], wa[:, 1, c:c + 1].broadcast_to([P, P]),
                                        ident[:, :], start=True, stop=True)
                    ins.then_inc(s_wa2t, 1)

            x_turn(0, 0)
            a_bcast()
            pe.wait_ge(s_const, 5)
            sweep(pe, tile1, 0, 1, NT, start=0)

            pe.wait_ge(s_bias, 32)
            for j in range(2):
                ins = pe.transpose(b_ps[:, j * E * KC:(j + 1) * E * KC], b_rows[:, j, :],
                                   ident[0:E * KC, 0:E * KC])
            ins.then_inc(s_bt, 1)

            def p_turn(t, par, b):
                R = rows(t)
                pe.wait_ge(s_prob, t + 1)
                after(pe, s_plo[b], t, 1)
                for k in range(BANKS3[b], BANKS3[b + 1]):
                    K = rows(k)
                    o = (k - BANKS3[b]) * P
                    ins = pe.transpose(pt_ps[b][0:K, o:o + R], prob[0:R, par, k * P:k * P + K], ident[0:R, 0:R])
                ins.then_inc(s_pt[b], 1)

            def attend(t, par, b):
                R = rows(t)
                pe.wait_ge(s_plo[b], t + 1)
                if b == 0:
                    after(pe, s_relu, t, 2)
                for k in range(BANKS3[b], BANKS3[b + 1]):
                    K = rows(k)
                    for n, (p, h) in enumerate(((pt_lo, h_hi), (pt_hi, h_lo), (pt_hi, h_hi))):
                        ins = pe.matmul(o_ps[par][0:R, :], p[0:K, par, k, 0:R], h[0:K, k, :],
                                        start=(k == 0 and n == 0), stop=(k == NT - 1 and n == 2))
                if b == 2:
                    ins.then_inc(s_o, 1)

            def x2_turn(t, par):
                R = rows(t)
                pe.wait_ge(s_xn2, t + 1)
                after(pe, s_x2, t, 1)
                for c in range(KC):
                    ins = pe.transpose(x2_ps[:, c * P:c * P + R], xn2[0:R, par, c * P:(c + 1) * P],
                                       ident[0:R, 0:R])
                ins.then_inc(s_x2t, 1)

            def logits(t, par):
                R = rows(t)
                pe.wait_ge(s_x2, t + 1)
                after(pe, s_lg, t, 1)
                for c in range(KC):
                    ins = pe.matmul(logit_ps[0:R, 0:E], x2t[:, par, c, 0:R], wr_s[:, c, :],
                                    start=(c == 0), stop=(c == KC - 1))
                ins.then_inc(s_logit, 1)

            def positions(t, par):
                R = rows(t)
                pe.wait_ge(s_onehot, t + 1)
                after(pe, s_count, t, 1)
                pe.matmul(pos_ps[0:R, 0:E], upto[0:R, 0:R], onehot[0:R, par, :], start=True, stop=False)
                pe.matmul(pos_ps[0:R, 0:E], ones[:, 0:R], counts[:, :], start=False, stop=True).then_inc(s_post, 1)

            def tile2(t, par):
                if isinstance(t, int) and t == 0:
                    attend(0, 0, 0)
                    attend(0, 0, 1)
                    for b in range(3):
                        p_turn(1, 1, b)
                    attend(0, 0, 2)
                    return
                if there(t + 1):
                    p_turn(t + 1, 1 - par, 0)
                if there(t):
                    attend(t, par, 0)
                if there(t - 2):
                    logits(t - 2, par)
                if there(t + 1):
                    p_turn(t + 1, 1 - par, 1)
                if there(t):
                    attend(t, par, 1)
                if there(t - 3):
                    positions(t - 3, 1 - par)
                if there(t + 1):
                    p_turn(t + 1, 1 - par, 2)
                if there(t):
                    attend(t, par, 2)
                if there(t - 1):
                    x2_turn(t - 1, 1 - par)

            pe.wait_ge(s_hlo, NT)
            pe.wait_ge(s_const, 10)
            pe.wait_ge(s_small, 32)
            for b in range(3):
                p_turn(0, 0, b)
            sweep(pe, tile2, 3, 2, NT, first=4, start=0)

            def in_turn(e, par):
                pe.wait_ge(s_in[par], landed(e, par, 32))
                after(pe, s_gxt, e, 1)
                for c in range(KC):
                    o = (c % 2) * CAP
                    for j, R in ((0, P), (1, CAP2)):
                        ins = pe.transpose(gx_ps[c // 2][:, o + j * P:o + j * P + R],
                                           dispatched[par][0:R, j, c * P:(c + 1) * P], ident[0:R, 0:R])
                ins.then_inc(s_gt, 1)

            def layer(ps, w, v, done):
                for f in range(KC):
                    for c in range(KC):
                        ins = pe.matmul(ps[f // 2][:, (f % 2) * CAP:(f % 2 + 1) * CAP],
                                        w[:, c, f * P:(f + 1) * P], v[:, c, :], start=(c == 0), stop=(c == KC - 1))
                    if f % 2 == 1:
                        ins.then_inc(done, 1)

            def first_layer(e, par):
                pe.wait_ge(s_w1[par], landed(e, par))
                pe.wait_ge(s_gxt, e + 1)
                after(pe, s_hidv, e, 1)
                layer(hid_ps, w1_s[:, par, :, :], gx_t[par], s_hid)

            def second_layer(e, par):
                pe.wait_ge(s_w2[par], landed(e, par))
                pe.wait_ge(s_hidv, e + 1)
                after(pe, s_eol, e, 1)
                after(pe, s_eov, e, 1)
                layer(eo_ps, w2_s[:, par, :, :], hid[par], s_eo)

            def out_turn(e, par):
                after_halves(pe, s_fin, e, 1)
                for half_, done in ((0, s_eol), (1, s_eov)):
                    pe.wait_ge(done, e + 1)
                    for j, R in ((0, P), (1, CAP2)):
                        for c in range(half_ * KC // 2, (half_ + 1) * KC // 2):
                            ins = pe.transpose(y_ps[j][0:R, c * P:(c + 1) * P], eo_t[par][:, c, j * P:j * P + R],
                                               ident[:, :])
                        if half_:
                            ins.then_inc(s_y, 1)

            def expert(e, par):
                if there(e, E):
                    first_layer(e, par)
                if there(e + 1, E):
                    in_turn(e + 1, 1 - par)
                if there(e - 1, E):
                    out_turn(e - 1, 1 - par)
                if there(e, E):
                    second_layer(e, par)

            sweep(pe, expert, 1, 1, E)


_INS = ["x", "adj", "L0_gnn_W", "L0_gnn_a1", "L0_gnn_a2", "L0_ffn_Wr", "L0_ffn_br", "L0_ffn_W1",
        "L0_ffn_b1", "L0_ffn_W2", "L0_ffn_b2"]


def kernel(**inputs):
    import numpy as _np
    import concourse.bacc as _bacc
    from concourse import mybir as _mybir
    from concourse.bass_utils import run_bass_kernel_spmd as _run

    nc = _bacc.Bacc("TRN2", target_bir_lowering=False, num_devices=1)
    arrays, args = {}, []
    for name in _INS:
        a = _np.ascontiguousarray(inputs[name])
        arrays[f"in_{name}_dram"] = a
        args.append(nc.dram_tensor(f"in_{name}_dram", a.shape, _mybir.dt.from_np(a.dtype), kind="ExternalInput").ap())
    shape = inputs["x"].shape
    args.append(nc.dram_tensor("out_0_dram", shape, _mybir.dt.float32, kind="ExternalOutput").ap())
    gat_moe(nc, *args)
    r = _run(nc, [arrays], core_ids=[0])
    return r.results[0]["out_0_dram"]
```
